# Optimizing a Trainium2 kernel written in Bass

```python
import numpy as np
import jax
import jax.numpy as jnp

def _softmax(x, axis=-1):
    return jax.nn.softmax(x, axis=axis)

def _gelu(x):
    return jax.nn.gelu(x, approximate=True)

def _silu(x):
    return jax.nn.silu(x)

def _sigmoid(x):
    return jax.nn.sigmoid(x)

def _layernorm(x, axis=-1, eps=1e-05):
    m = jnp.mean(x, axis=axis, keepdims=True)
    v = jnp.var(x, axis=axis, keepdims=True)
    return (x - m) / jnp.sqrt(v + eps)

def _scatter_add(tgt, idx, src, axis=0):
    return tgt.at[idx].add(src)

def _segment_sum(src, seg, n):
    return jax.ops.segment_sum(src, seg, n)
kernel_name = 'mk_adaln_d1_jaxref_r8_21106e'

def setup_inputs(seed: int=0):
    np.random.seed(seed)
    _w = jnp.asarray

    def _L0_attn_setup():
        import jax, jax.numpy as jnp
        import numpy as np
        N, L, D, A, F, B = (4, 512, 128, 128, 512, 8)
        EPS_LN = 1e-06
        EPS_Z = 1e-06

        def _layernorm(x, scale, bias):
            m = jnp.mean(x, axis=-1, keepdims=True)
            v = jnp.mean(jnp.square(x - m), axis=-1, keepdims=True)
            return (x - m) * jax.lax.rsqrt(v + EPS_LN) * scale + bias

        def _block(x, p):
            Wq, bq, Wk, bk, Wv, bv, Wo, bo, ln1_s, ln1_b, Wf1, bf1, Wf2, bf2, ln2_s, ln2_b = p
            residual = x
            q = jnp.einsum('nld,da->nla', x, Wq) + bq
            k = jnp.einsum('nld,da->nla', x, Wk) + bk
            v = jnp.einsum('nld,da->nla', x, Wv) + bv
            Q = jax.nn.elu(q) + 1.0
            K = jax.nn.elu(k) + 1.0
            KV = jnp.einsum('nsh,nsh->nh', K, v)
            Ksum = jnp.sum(K, axis=1)
            Z = 1.0 / (Q * Ksum[:, None, :] + EPS_Z)
            V = Q * KV[:, None, :] * Z
            attn = jax.nn.gelu(jnp.einsum('nla,ad->nld', V, Wo) + bo)
            x = _layernorm(attn + residual, ln1_s, ln1_b)
            residual = x
            h = jax.nn.gelu(jnp.einsum('nld,df->nlf', x, Wf1) + bf1)
            ff = jax.nn.gelu(jnp.einsum('nlf,fd->nld', h, Wf2) + bf2)
            x = _layernorm(ff + residual, ln2_s, ln2_b)
            return (x, None)
        key = jax.random.key(seed)
        ks = jax.random.split(key, 10)
        s = 0.02
        x = jax.random.normal(ks[0], (N, L, D), dtype=jnp.float32)
        Wq = jax.random.normal(ks[1], (B, D, A), dtype=jnp.float32) * s
        Wk = jax.random.normal(ks[2], (B, D, A), dtype=jnp.float32) * s
        Wv = jax.random.normal(ks[3], (B, D, A), dtype=jnp.float32) * s
        Wo = jax.random.normal(ks[4], (B, A, D), dtype=jnp.float32) * s
        Wf1 = jax.random.normal(ks[5], (B, D, F), dtype=jnp.float32) * s
        Wf2 = jax.random.normal(ks[6], (B, F, D), dtype=jnp.float32) * s
        return {'x': x, 'Wq': Wq, 'bq': jnp.zeros((B, A), jnp.float32), 'Wk': Wk, 'bk': jnp.zeros((B, A), jnp.float32), 'Wv': Wv, 'bv': jnp.zeros((B, A), jnp.float32), 'Wo': Wo, 'bo': jnp.zeros((B, D), jnp.float32), 'ln1_s': jnp.ones((B, D), jnp.float32), 'ln1_b': jnp.zeros((B, D), jnp.float32), 'Wf1': Wf1, 'bf1': jnp.zeros((B, F), jnp.float32), 'Wf2': Wf2, 'bf2': jnp.zeros((B, D), jnp.float32), 'ln2_s': jnp.ones((B, D), jnp.float32), 'ln2_b': jnp.zeros((B, D), jnp.float32)}
    _L0_attn_in = _L0_attn_setup()

    def _L0_ffn_setup():
        import jax, jax.numpy as jnp
        import numpy as np
        TOP_K = 2
        key = jax.random.key(seed)
        ks = jax.random.split(key, 8)
        B, S, H, F, E = (1, 128, 128, 128, 8)
        Fs = 2 * F
        s = lambda k, shape, scale: jax.random.normal(k, shape, dtype=jnp.float32) * scale
        return {'x': s(ks[0], (B, S, H), 1.0), 'router_w': s(ks[1], (H, E), 0.02), 'gate_w': s(ks[2], (E, H, F), 0.02), 'up_w': s(ks[3], (E, H, F), 0.02), 'down_w': s(ks[4], (E, F, H), 0.02), 'shared_gate_w': s(ks[5], (H, Fs), 0.02), 'shared_up_w': s(ks[6], (H, Fs), 0.02), 'shared_down_w': s(ks[7], (Fs, H), 0.02)}
    _L0_ffn_in = _L0_ffn_setup()
    _L0_c = _w((lambda *s: np.random.randn(*s).astype(np.float32) * 0.05)(8, 128))
    _L0_wmod = _w((lambda *s: np.random.randn(*s).astype(np.float32) * 0.05)(128, 6 * 128) * 128 ** (-0.5))
    _d = {'L0_attn_x': _L0_attn_in['x'], 'L0_attn_Wq': _L0_attn_in['Wq'], 'L0_attn_bq': _L0_attn_in['bq'], 'L0_attn_Wk': _L0_attn_in['Wk'], 'L0_attn_bk': _L0_attn_in['bk'], 'L0_attn_Wv': _L0_attn_in['Wv'], 'L0_attn_bv': _L0_attn_in['bv'], 'L0_attn_Wo': _L0_attn_in['Wo'], 'L0_attn_bo': _L0_attn_in['bo'], 'L0_attn_ln1_s': _L0_attn_in['ln1_s'], 'L0_attn_ln1_b': _L0_attn_in['ln1_b'], 'L0_attn_Wf1': _L0_attn_in['Wf1'], 'L0_attn_bf1': _L0_attn_in['bf1'], 'L0_attn_Wf2': _L0_attn_in['Wf2'], 'L0_attn_bf2': _L0_attn_in['bf2'], 'L0_attn_ln2_s': _L0_attn_in['ln2_s'], 'L0_attn_ln2_b': _L0_attn_in['ln2_b'], 'L0_ffn_router_w': _L0_ffn_in['router_w'], 'L0_ffn_gate_w': _L0_ffn_in['gate_w'], 'L0_ffn_up_w': _L0_ffn_in['up_w'], 'L0_ffn_down_w': _L0_ffn_in['down_w'], 'L0_ffn_shared_gate_w': _L0_ffn_in['shared_gate_w'], 'L0_ffn_shared_up_w': _L0_ffn_in['shared_up_w'], 'L0_ffn_shared_down_w': _L0_ffn_in['shared_down_w'], 'L0_c': _L0_c, 'L0_wmod': _L0_wmod}
    _x0 = _d['L0_attn_x']
    _d['L0_attn_x'] = jax.random.normal(jax.random.fold_in(jax.random.key(seed), 1), (8, 256, 128), dtype=_x0.dtype)
    del _x0
    return _d

def reference(L0_attn_x, L0_attn_Wq, L0_attn_bq, L0_attn_Wk, L0_attn_bk, L0_attn_Wv, L0_attn_bv, L0_attn_Wo, L0_attn_bo, L0_attn_ln1_s, L0_attn_ln1_b, L0_attn_Wf1, L0_attn_bf1, L0_attn_Wf2, L0_attn_bf2, L0_attn_ln2_s, L0_attn_ln2_b, L0_ffn_router_w, L0_ffn_gate_w, L0_ffn_up_w, L0_ffn_down_w, L0_ffn_shared_gate_w, L0_ffn_shared_up_w, L0_ffn_shared_down_w, L0_c, L0_wmod):

    def _L0_attn_ref(x, Wq, bq, Wk, bk, Wv, bv, Wo, bo, ln1_s, ln1_b, Wf1, bf1, Wf2, bf2, ln2_s, ln2_b):
        import jax, jax.numpy as jnp
        import numpy as np
        N, L, D, A, F, B = (4, 512, 128, 128, 512, 8)
        EPS_LN = 1e-06
        EPS_Z = 1e-06

        def _layernorm(x, scale, bias):
            m = jnp.mean(x, axis=-1, keepdims=True)
            v = jnp.mean(jnp.square(x - m), axis=-1, keepdims=True)
            return (x - m) * jax.lax.rsqrt(v + EPS_LN) * scale + bias

        def _block(x, p):
            Wq, bq, Wk, bk, Wv, bv, Wo, bo, ln1_s, ln1_b, Wf1, bf1, Wf2, bf2, ln2_s, ln2_b = p
            residual = x
            q = jnp.einsum('nld,da->nla', x, Wq) + bq
            k = jnp.einsum('nld,da->nla', x, Wk) + bk
            v = jnp.einsum('nld,da->nla', x, Wv) + bv
            Q = jax.nn.elu(q) + 1.0
            K = jax.nn.elu(k) + 1.0
            KV = jnp.einsum('nsh,nsh->nh', K, v)
            Ksum = jnp.sum(K, axis=1)
            Z = 1.0 / (Q * Ksum[:, None, :] + EPS_Z)
            V = Q * KV[:, None, :] * Z
            attn = jax.nn.gelu(jnp.einsum('nla,ad->nld', V, Wo) + bo)
            x = _layernorm(attn + residual, ln1_s, ln1_b)
            residual = x
            h = jax.nn.gelu(jnp.einsum('nld,df->nlf', x, Wf1) + bf1)
            ff = jax.nn.gelu(jnp.einsum('nlf,fd->nld', h, Wf2) + bf2)
            x = _layernorm(ff + residual, ln2_s, ln2_b)
            return (x, None)
        params = (Wq, bq, Wk, bk, Wv, bv, Wo, bo, ln1_s, ln1_b, Wf1, bf1, Wf2, bf2, ln2_s, ln2_b)
        out, _ = jax.lax.scan(_block, x, params)
        return out

    def _L0_ffn_ref(x, router_w, gate_w, up_w, down_w, shared_gate_w, shared_up_w, shared_down_w):
        import jax, jax.numpy as jnp
        import numpy as np
        TOP_K = 2
        B, S, H = x.shape
        N = B * S
        xf = x.reshape(N, H)
        scores = jax.nn.softmax(xf @ router_w, axis=-1)
        topk_scores, topk_idx = jax.lax.top_k(scores, TOP_K)
        E = scores.shape[-1]
        combine = jnp.zeros((N, E), dtype=x.dtype).at[jnp.arange(N)[:, None], topk_idx].add(topk_scores)
        g = jnp.einsum('nh,ehf->enf', xf, gate_w)
        u = jnp.einsum('nh,ehf->enf', xf, up_w)
        y = jnp.einsum('enf,efh->enh', jax.nn.silu(g) * u, down_w)
        routed = jnp.einsum('enh,ne->nh', y, combine)
        shared = jax.nn.silu(xf @ shared_gate_w) * (xf @ shared_up_w) @ shared_down_w
        return (shared + routed).reshape(B, S, H)
    x = L0_attn_x
    mod = (_silu(L0_c) @ L0_wmod).reshape(L0_c.shape[0], 6, 1, -1)
    sa, ca, ga, sb, cb, gb = (mod[:, 0], mod[:, 1], mod[:, 2], mod[:, 3], mod[:, 4], mod[:, 5])
    ga = (2 * (ga >= 0) - 1) * jnp.maximum(jnp.abs(ga), 0.25)
    gb = (2 * (gb >= 0) - 1) * jnp.maximum(jnp.abs(gb), 0.25)
    h = _layernorm(x, axis=-1) * (1 + ca) + sa
    x = x + ga * _L0_attn_ref(h, L0_attn_Wq, L0_attn_bq, L0_attn_Wk, L0_attn_bk, L0_attn_Wv, L0_attn_bv, L0_attn_Wo, L0_attn_bo, L0_attn_ln1_s, L0_attn_ln1_b, L0_attn_Wf1, L0_attn_bf1, L0_attn_Wf2, L0_attn_bf2, L0_attn_ln2_s, L0_attn_ln2_b)
    h = _layernorm(x, axis=-1) * (1 + cb) + sb
    x = x + gb * _L0_ffn_ref(h, L0_ffn_router_w, L0_ffn_gate_w, L0_ffn_up_w, L0_ffn_down_w, L0_ffn_shared_gate_w, L0_ffn_shared_up_w, L0_ffn_shared_down_w)
    return x

_drawn_inputs = setup_inputs


def setup_inputs(seed=0):
    import zlib

    import numpy as np

    out = dict(_drawn_inputs(seed))
    spreads = {'L0_attn_bq': (0.0, 2.0),
     'L0_attn_bk': (0.0, 0.8),
     'L0_attn_bv': (0.0, 0.8),
     'L0_attn_bo': (0.0, 0.1),
     'L0_attn_ln1_s': (1.0, 0.2),
     'L0_attn_ln1_b': (0.0, 0.1),
     'L0_attn_bf1': (0.0, 0.8),
     'L0_attn_bf2': (0.0, 0.1),
     'L0_attn_ln2_s': (1.0, 0.2),
     'L0_attn_ln2_b': (0.0, 0.1)}
    factors = {'L0_attn_Wq': 64.0,
     'L0_attn_Wk': 8.0,
     'L0_attn_Wv': 8.0,
     'L0_attn_Wo': 6.46,
     'L0_attn_Wf1': 2.947,
     'L0_ffn_router_w': 8.0,
     'L0_ffn_gate_w': 8.0,
     'L0_ffn_up_w': 8.0,
     'L0_ffn_down_w': 8.0,
     'L0_ffn_shared_gate_w': 8.0,
     'L0_ffn_shared_up_w': 8.0,
     'L0_ffn_shared_down_w': 8.0}
    for name, (base, spread) in spreads.items():
        noise = np.random.default_rng([zlib.crc32(name.encode()), seed]).standard_normal(out[name].shape)
        drawn = base * np.exp(spread * noise) if base else spread * noise
        out[name] = jnp.asarray(drawn.astype(out[name].dtype))
    for name, factor in factors.items():
        out[name] = (out[name] * factor).astype(out[name].dtype)
    return out
```

```python
import math
from contextlib import ExitStack

import concourse.bass as bass
from concourse import mybir

ALU = mybir.AluOpType
ACT = mybir.ActivationFunctionType
F32 = mybir.dt.float32
BF16 = mybir.dt.bfloat16
AX_X = mybir.AxisListType.X

P = 128
NB, L, D = 8, 256, 128
LAYERS, F = 8, 512
E = 8
G = 512
CH = NB * L // G
HB = G // L
T = G // P
FJ = F // P
NI = LAYERS * CH
U = E + 2
EPS_LN, EPS_Z, EPS_MOD = 1e-6, 1e-6, 1e-5
LN_SET = "natural_log_exp_and_others"


def adaln_block(nc, x, w_qkv, w_o, w_f1, w_f2, v_a, v_bo, v_ln1, v_bf1, v_bf2, v_ln2, c_t, w_mod,
                w_router, w_unit, ident_in, select_in, lower_in, out):
    with ExitStack() as ctx:
        def sb(name, shape, dt=F32):
            return ctx.enter_context(nc.sbuf_tensor(name, shape, dt))

        def sem(name):
            return ctx.enter_context(nc.semaphore(name))

        ident = sb("ident", [P, P])
        wqkv = sb("wqkv", [P, 3 * P])
        wo = sb("wo", [P, P])
        wf1 = sb("wf1", [P, F])
        wf2 = sb("wf2", [P, FJ, P])
        va = sb("va", [P, 3])
        vbo = sb("vbo", [P, 1])
        vln1 = sb("vln1", [P, 2])
        vbf1 = sb("vbf1", [P, FJ])
        vbf2 = sb("vbf2", [P, 1])
        vln2 = sb("vln2", [P, 2])
        x0 = sb("x0", [P, CH, T, D])
        xs = [sb(f"xs{c}", [P, G]) for c in range(CH)]
        x2 = [sb(f"x2_{c}", [P, G]) for c in range(CH)]
        vt = [sb(f"vt{c}", [P, G]) for c in range(CH)]
        ek, eq = sb("ek", [P, G]), sb("eq", [P, G])
        mk, mq = sb("mk", [P, G]), sb("mq", [P, G])
        kk, qq, kv_full = sb("kk", [P, G]), sb("qq", [P, G]), sb("kv_full", [P, G])
        lden, dd = sb("lden", [P, G]), sb("dd", [P, G])
        rk_elu, rq_elu, kpos = sb("elu_k_fm", [P, G]), sb("elu_q_fm", [P, G]), sb("kpos", [P, HB])
        ksum, kvsum, rk = sb("ksum", [P, HB]), sb("kvsum", [P, HB]), sb("rk", [P, HB])
        ck, nck = sb("ck", [P, HB]), sb("nck", [P, HB])
        g1, y1, g2, y2 = sb("g1", [P, G]), sb("y1", [P, G]), sb("g2", [P, G]), sb("y2", [P, G])
        hid = sb("hid", [P, FJ, G])
        xh = {k: sb(f"xh{k}", [P, T, D]) for k in "IBDF"}
        st = {k: sb(f"st{k}", [P, T, 6]) for k in "IBDF"}
        dif, mn, sq, dif2, mean = ({k: sb(f"{name}{k}", [P, T]) for k in "IBDF"}
                                   for name in ("dif", "mn", "sq", "dif2", "mean"))
        ve = {k: sb(f"ve{k}", [P, T]) for k in "IBDF"}
        rs = {k: sb(f"rs{k}", [P, T]) for k in "IBDF"}
        c_eps, c_lneps, c_half = sb("c_eps", [P, 1]), sb("c_lneps", [P, 1]), sb("c_half", [P, T])
        ct, sct = sb("ct", [P, NB]), sb("sct", [P, NB])
        wmod = sb("wmod", [P, 6 * D])
        mod = sb("mod", [P, 6, NB])
        m1 = sb("m1", [P, 2, NB])
        gt = sb("gt", [P, 2, NB])
        gsg, gab = sb("gsg", [P, 2, NB]), sb("gab", [P, 2, NB])
        wr = sb("wr", [P, E])
        wu = sb("wu", [P, U, 3, P])
        sel32, sel = sb("sel32", [3 * E, E * P]), sb("sel", [3 * E, E * P], BF16)
        lower = sb("lower", [P, E * E])
        zf = sb("zf", [P, G])
        hf = [sb(f"hf{c}", [P, G]) for c in range(CH)]
        mx, lg, ex = sb("mx", [P, T]), sb("lg", [P, T, E]), sb("ex", [P, T, E])
        sm, rsm = sb("sm", [P, T]), sb("rsm", [P, T])
        cmp_gt, cmp_eq = sb("cmp_gt", [P, T, E * E]), sb("cmp_eq", [P, T, E * E])
        cmp_lo, cmp_all = sb("cmp_lo", [P, T, E * E]), sb("cmp_all", [P, T, E * E])
        rank, comb, comb2 = sb("rank", [P, T, E]), sb("comb", [P, T, E]), sb("comb2", [P, T, E])
        res1, res2 = sb("res1", [P, T, E]), sb("res2", [P, T, E])
        cs = sb("cs", [P, T, 3, E], BF16)
        identb = sb("identb", [P, P], BF16)
        cst = [sb(f"cst{c}", [3 * E, G], BF16) for c in range(CH)]
        sg = [sb(f"sg{i}", [P, G]) for i in range(2)]
        su = [sb(f"su{i}", [P, G]) for i in range(2)]
        sc = [sb(f"sc{i}", [P, G]) for i in range(2)]
        yf = sb("yf", [P, G])
        ot = [sb(f"ot{i}", [P, T, D]) for i in range(2)]

        bank = [ctx.enter_context(nc.psum_tensor(f"bank{i}", [P, G], F32)) for i in range(8)]
        ps_k, ps_q, ps_v, ps_f0, ps_f1, ps_b, ps_d, ps_y = bank
        ps_ff = [ps_f0, ps_f1, ps_k, ps_v]

        ld = {k: sem(f"ld_{k}") for k in ("const", "mod", "moe", "wqkv", "va", "wo", "vbo", "vln1",
                                          "wf1", "vbf1", "wf2", "vbf2", "vln2")}
        ld["x0"] = [sem(f"ld_x0_{c}") for c in range(CH)]
        consts_set = sem("consts_set")
        silu_c, mod_mm, mod_copied, mod_done = sem("silu_c"), sem("mod_mm"), sem("mod_copied"), sem("mod_done")
        ga_parts = sem("ga_parts")
        k_mm, q_mm, v_mm = sem("k_mm"), sem("q_mm"), sem("v_mm")
        ek_ready, eq_ready = sem("ek_ready"), sem("eq_ready")
        elu_k, elu_q, kpos_ready = sem("elu_k"), sem("elu_q"), sem("kpos_ready")
        mk_ready, k_ready, mq_ready, q_ready = sem("mk_ready"), sem("k_ready"), sem("mq_ready"), sem("q_ready")
        rk_ready, kv_ready, ck_ready, nck_ready = sem("rk_ready"), sem("kv_ready"), sem("ck_ready"), sem("nck_ready")
        lden_ready, dd_ready, v_ready = sem("lden_ready"), sem("dd_ready"), sem("v_ready")
        wo_mm, g1_ready, y1_ready = sem("wo_mm"), sem("g1_ready"), sem("y1_ready")
        ff1_mm, h_ready, ff2_mm, g2_ready, y2_ready = (sem("ff1_mm"), sem("h_ready"), sem("ff2_mm"),
                                                       sem("g2_ready"), sem("y2_ready"))
        x2_ready, x_ready = sem("x2_ready"), sem("x_ready")
        to_tm = {k: sem(f"to_tm{k}") for k in "BDF"}
        bn_done = {k: sem(f"bn_done{k}") for k in "IBDF"}
        agg_done = {k: sem(f"agg_done{k}") for k in "IBDF"}
        var_ready = {k: sem(f"var_ready{k}") for k in "IBDF"}
        rstd_ready = {k: sem(f"rstd_ready{k}") for k in "IBDF"}
        normed = {k: sem(f"normed{k}") for k in "IBDF"}
        to_fm = {k: sem(f"to_fm{k}") for k in "IBDF"}
        zf_ready, x_new, hf_ready = sem("zf_ready"), sem("x_new"), sem("hf_ready")
        moe_consts, score_mm, mx_ready, lg_ready, ex_ready = (sem("moe_consts"), sem("score_mm"), sem("mx_ready"),
                                                              sem("lg_ready"), sem("ex_ready"))
        rt = sem("rt")
        cs_ready, cst_mm, cst_ready = sem("cs_ready"), sem("cst_mm"), sem("cst_ready")
        gate_mm, up_mm, bc_mm, down_mm = sem("gate_mm"), sem("up_mm"), sem("bc_mm"), sem("down_mm")
        sg_ready, su_ready, sc_ready = sem("sg_ready"), sem("su_ready"), sem("sc_ready")
        yf_ready, out_tm, ot_ready, stored = sem("yf_ready"), sem("out_tm"), sem("ot_ready"), [sem(f"stored{i}") for i in range(2)]

        x_rows = x.rearrange("(c h p j) d -> p c h j d", c=CH, h=HB, p=P)
        out_rows = out.rearrange("(c h p j) d -> p c h j d", c=CH, h=HB, p=P)

        def half(ap, h):
            return ap[:, h * L:(h + 1) * L]

        def has(n):
            return not isinstance(n, int) or 0 <= n < NI

        def wait(eng, s, value):
            if not isinstance(value, int) or value > 0:
                eng.wait_ge(s, value)

        def routed(i):
            return i // U * E + min(i % U, E)

        def slots(eng, one_slot):
            for s in range(CH - 1):
                one_slot(s, s % CH, s // CH)
            with eng.Fori(0, LAYERS - 1) as i:
                for j in range(CH):
                    s = CH - 1 + j
                    one_slot(i * CH + s, s % CH, i + s // CH)
            for s in range(NI - 1, NI + CH - 1):
                one_slot(s, s % CH, s // CH)

        block = ctx.enter_context(nc.Block())

        @block.sync
        def _(sp):
            sp.dma_start(ident[:], ident_in).then_inc(ld["const"], 16)
            for c in range(CH):
                sp.dma_start(x0[:, c, :, :].rearrange("p (h j) d -> p h j d", h=HB), x_rows[:, c]).then_inc(ld["x0"][c], 16)
            sp.dma_start(ct[:], c_t).then_inc(ld["mod"], 16)
            sp.dma_start(wmod[:], w_mod).then_inc(ld["mod"], 16)

            def layer_loads(l, first):
                if not first:
                    sp.wait_ge(v_mm, CH * l)
                sp.dma_start(wqkv[:], w_qkv[l]).then_inc(ld["wqkv"], 16)
                if not first:
                    sp.wait_ge(kv_ready, CH * l)
                    sp.wait_ge(elu_q, CH * l)
                sp.dma_start(va[:], v_a[l]).then_inc(ld["va"], 16)
                if not first:
                    sp.wait_ge(wo_mm, CH * l)
                sp.dma_start(wo[:], w_o[l]).then_inc(ld["wo"], 16)
                if not first:
                    sp.wait_ge(g1_ready, CH * l)
                sp.dma_start(vbo[:], v_bo[l]).then_inc(ld["vbo"], 16)
                if not first:
                    sp.wait_ge(x2_ready, CH * l)
                sp.dma_start(vln1[:], v_ln1[l]).then_inc(ld["vln1"], 16)
                if not first:
                    sp.wait_ge(ff1_mm, FJ * CH * l)
                sp.dma_start(wf1[:], w_f1[l]).then_inc(ld["wf1"], 16)
                if not first:
                    sp.wait_ge(h_ready, FJ * CH * l)
                sp.dma_start(vbf1[:], v_bf1[l]).then_inc(ld["vbf1"], 16)
                if not first:
                    sp.wait_ge(ff2_mm, CH * l)
                sp.dma_start(wf2[:], w_f2[l]).then_inc(ld["wf2"], 16)
                if not first:
                    sp.wait_ge(g2_ready, CH * l)
                sp.dma_start(vbf2[:], v_bf2[l]).then_inc(ld["vbf2"], 16)
                if not first:
                    sp.wait_ge(x_ready, CH * l + CH)
                sp.dma_start(vln2[:], v_ln2[l]).then_inc(ld["vln2"], 16)

            layer_loads(0, True)
            sp.dma_start(wr[:], w_router).then_inc(ld["moe"], 16)
            sp.dma_start(sel32[:], select_in).then_inc(ld["moe"], 16)
            sp.dma_start(lower[:], lower_in).then_inc(ld["moe"], 16)
            for u in range(U):
                sp.dma_start(wu[:, u], w_unit[:, u]).then_inc(ld["moe"], 16)
            with sp.Fori(1, LAYERS) as l:
                layer_loads(l, False)
            for c in range(CH):
                sp.wait_ge(ot_ready, c + 1)
                sp.dma_start(out_rows[:, c], ot[c % 2][:, :, :].rearrange("p (h j) d -> p h j d", h=HB)).then_inc(stored[c % 2], 16)
            for i in range(2):
                sp.wait_ge(stored[i], 16 * CH // 2)

        MOE_LOADS = 16 * (3 + U)

        @block.tensor
        def _(pe):
            def transposes(out_bank, src, done):
                for j in range(T):
                    t = src[:, j, :] if len(src.shape) == 3 else src[:, j * P:(j + 1) * P]
                    mm = nc.tensor.transpose(out_bank[:, j * P:(j + 1) * P], t, ident[:])
                mm.then_inc(done, 1)

            pe.wait_ge(ld["const"], 16)
            pe.wait_ge(ld["mod"], 32)
            pe.wait_ge(silu_c, 1)
            for m in range(6):
                mm = nc.tensor.matmul(ps_y[:, m * NB:(m + 1) * NB], wmod[:, m * D:(m + 1) * D], sct[:],
                                      start=True, stop=True)
            mm.then_inc(mod_mm, 1)
            for c in range(CH):
                pe.wait_ge(normed["I"], c + 1)
                transposes([ps_f0, ps_f1, ps_b, ps_d][c], xh["I"], to_fm["I"])

            def slot(s, c, l):
                a, b, f, d = s, s - 1, s - 2, s - 3
                if has(a):
                    pe.wait_ge(x_ready, a + 1)
                    if c == 0:
                        pe.wait_ge(ld["wqkv"], 4 * a + 16)
                    if has(a - 3):
                        pe.wait_ge(h_ready, 4 * (a - 3) + 3)
                    elif has(a - 1):
                        pe.wait_ge(k_ready, a)
                    nc.tensor.matmul(ps_k[:], wqkv[:, 0:P], xs[c][:], start=True, stop=True).then_inc(k_mm, 1)
                    if has(a - 1):
                        pe.wait_ge(elu_q, a)
                    nc.tensor.matmul(ps_q[:], wqkv[:, P:2 * P], xs[c][:], start=True, stop=True).then_inc(q_mm, 1)
                    if has(a - 3):
                        pe.wait_ge(h_ready, 4 * (a - 3) + 4)
                    elif has(a - 1):
                        pe.wait_ge(kv_ready, a)
                    nc.tensor.matmul(ps_v[:], wqkv[:, 2 * P:3 * P], xs[c][:], start=True, stop=True).then_inc(v_mm, 1)
                if has(b):
                    pe.wait_ge(v_ready, b + 1)
                    if (c - 1) % CH == 0:
                        pe.wait_ge(ld["wo"], 4 * b + 16)
                    wait(pe, normed["B"], b)
                    if isinstance(b, int) and b == 0:
                        pe.wait_ge(x_ready, CH)
                    nc.tensor.matmul(ps_b[:], wo[:], vt[(c - 1) % CH][:], start=True, stop=True).then_inc(wo_mm, 1)
                if has(f):
                    pe.wait_ge(normed["B"], f + 1)
                    if has(f - 1):
                        pe.wait_ge(h_ready, 4 * (f - 1) + 1)
                    transposes(ps_f0, xh["B"], to_fm["B"])
                if has(d):
                    pe.wait_ge(y2_ready, d + 1)
                    pe.wait_ge(x_ready, d + CH)
                    transposes(ps_d, y2, to_tm["D"])
                if has(f):
                    pe.wait_ge(x2_ready, f + 1)
                    if (c - 2) % CH == 0:
                        pe.wait_ge(ld["wf1"], 4 * f + 16)
                    for j in range(FJ):
                        if j == 1 and has(f - 1):
                            pe.wait_ge(h_ready, 4 * (f - 1) + 2)
                        if j == 2:
                            pe.wait_ge(k_ready, a + 1 if has(a) else NI)
                            if not has(a):
                                pe.wait_ge(h_ready, 4 * (f - 1) + 3)
                        if j == 3:
                            pe.wait_ge(kv_ready, a + 1 if has(a) else NI)
                            if not has(a):
                                pe.wait_ge(h_ready, 4 * (f - 1) + 4)
                        nc.tensor.matmul(ps_ff[j][:], wf1[:, j * P:(j + 1) * P], x2[(c - 2) % CH][:],
                                         start=True, stop=True).then_inc(ff1_mm, 1)
                if has(d):
                    pe.wait_ge(normed["D"], d + 1)
                    transposes(ps_d, xh["D"], to_fm["D"])
                for j in range(FJ):
                    if has(f):
                        if j == 0:
                            if (c - 2) % CH == 0:
                                pe.wait_ge(ld["wf2"], 4 * f + 16)
                            wait(pe, g2_ready, f)
                            if isinstance(f, int) and f == 0:
                                pe.wait_ge(mod_copied, 1)
                        pe.wait_ge(h_ready, 4 * f + j + 1)
                        mm = nc.tensor.matmul(ps_y[:], wf2[:, j, :], hid[:, j, :], start=(j == 0), stop=(j == FJ - 1))
                        if j == FJ - 1:
                            mm.then_inc(ff2_mm, 1)
                    if j == 1 and has(b):
                        pe.wait_ge(y1_ready, b + 1)
                        transposes(ps_b, y1, to_tm["B"])

            slots(pe, slot)

            def prep(c):
                pe.wait_ge(zf_ready, c + 1)
                if c:
                    pe.wait_ge(hf_ready, c)
                transposes(ps_b, zf, to_tm["F"])
                pe.wait_ge(normed["F"], c + 1)
                transposes(ps_b, xh["F"], to_fm["F"])
                pe.wait_ge(hf_ready, c + 1)
                if c:
                    pe.wait_ge(cst_ready, c)
                for j in range(T):
                    mm = nc.tensor.matmul(ps_d[:, j * E:(j + 1) * E], hf[c][:, j * P:(j + 1) * P], wr[:],
                                          start=True, stop=True)
                mm.then_inc(score_mm, 1)
                pe.wait_ge(cs_ready, c + 1)
                psb = ps_d[:].bitcast(BF16)
                for j in range(T):
                    mm = nc.tensor.transpose(psb[0:3 * E, j * P:(j + 1) * P],
                                             cs[:, j, :, :].rearrange("p a e -> p (a e)"), identb[:])
                mm.then_inc(cst_mm, 1)

            pe.wait_ge(ld["moe"], MOE_LOADS)
            pe.wait_ge(moe_consts, 2)
            for c in range(CH):
                prep(c)

            def down(i):
                c, u = divmod(i, U)
                if u < E:
                    pe.wait_ge(sc_ready, routed(i) + 1)
                else:
                    pe.wait_ge(su_ready, i + 1)
                if u == 0 and c:
                    pe.wait_ge(yf_ready, HB * c)
                mm = nc.tensor.matmul(ps_y[:], wu[:, u, 2, :], sc[i % 2][:], start=(u == 0), stop=(u == U - 1))
                mm.then_inc(down_mm, 1)

            def finish(c):
                pe.wait_ge(yf_ready, HB * (c + 1))
                if c:
                    pe.wait_ge(ot_ready, c)
                transposes(ps_b, yf, out_tm)

            gb = [ps_k, ps_q]
            ub = [ps_v, ps_f0]
            for i in range(CH * U):
                c, u = divmod(i, U)
                if u == 0:
                    pe.wait_ge(hf_ready, c + 1)
                if i >= 2:
                    pe.wait_ge(sg_ready, i - 1)
                nc.tensor.matmul(gb[i % 2][:], wu[:, u, 0, :], hf[c][:], start=True, stop=True).then_inc(gate_mm, 1)
                if i >= 2:
                    pe.wait_ge(su_ready, i - 1)
                nc.tensor.matmul(ub[i % 2][:], wu[:, u, 1, :], hf[c][:], start=True, stop=True).then_inc(up_mm, 1)
                if u < E:
                    if u == 0:
                        pe.wait_ge(cst_ready, c + 1)
                    if i:
                        pe.wait_ge(sc_ready, routed(i))
                    nc.tensor.matmul(ps_f1[:], sel[:, u * P:(u + 1) * P], cst[c][:], start=True, stop=True).then_inc(bc_mm, 1)
                if i:
                    down(i - 1)
                if u == 1 and c:
                    finish(c - 1)
            down(CH * U - 1)
            finish(CH - 1)

        @block.scalar
        def _(act):
            act.wait_ge(ld["mod"], 32)
            nc.scalar.activation(sct[:], ct[:], ACT.Silu).then_inc(silu_c, 1)
            act.wait_ge(mod_done, 1)
            for c in range(CH):
                act.wait_ge(to_fm["I"], c + 1)
                for h in range(HB):
                    b = c * HB + h
                    ev = nc.scalar.activation(half(xs[c], h), half([ps_f0, ps_f1, ps_b, ps_d][c], h), ACT.Identity,
                                              bias=mod[:, 0, b:b + 1], scale=m1[:, 0, b:b + 1])
                ev.then_inc(x_ready, 1)
            act.wait_ge(consts_set, 3)

            def slot(s, c, l):
                a, b, f, d = s, s - 1, s - 2, s - 3
                if has(d):
                    act.wait_ge(ff2_mm, d + 1)
                    if (c - 3) % CH == 0:
                        act.wait_ge(ld["vbf2"], 4 * d + 16)
                    nc.scalar.activation(g2[:], ps_y[:], ACT.Gelu_apprx_tanh, bias=vbf2[:, 0:1]).then_inc(g2_ready, 1)
                if has(a):
                    nc.scalar.preload_act_table_set(LN_SET)
                    act.wait_ge(k_mm, a + 1)
                    if c == 0:
                        act.wait_ge(ld["va"], 4 * a + 16)
                    nc.scalar.activation(ek[:], ps_k[:], ACT.Exp, bias=va[:, 0:1]).then_inc(ek_ready, 1)
                    act.wait_ge(q_mm, a + 1)
                    nc.scalar.activation(eq[:], ps_q[:], ACT.Exp, bias=va[:, 1:2]).then_inc(eq_ready, 1)
                if has(f):
                    act.wait_ge(to_fm["B"], f + 1)
                    if (c - 2) % CH == 0:
                        act.wait_ge(ld["vln1"], 4 * f + 16)
                    nc.scalar.activation(x2[(c - 2) % CH][:], ps_f0[:], ACT.Identity,
                                         bias=vln1[:, 1:2], scale=vln1[:, 0:1]).then_inc(x2_ready, 1)
                if has(a):
                    act.wait_ge(k_ready, a + 1)
                    act.wait_ge(q_ready, a + 1)
                    for h in range(HB):
                        ln = nc.scalar.activation(half(lden, h), half(qq, h), ACT.Ln,
                                                  bias=c_eps[:, 0:1], scale=ksum[:, h:h + 1])
                    ln.then_inc(lden_ready, 1)
                    act.wait_ge(lden_ready, a + 1)
                    nc.scalar.activation(dd[:], lden[:], ACT.Exp, bias=c_lneps[:, 0:1], scale=-1.0).then_inc(dd_ready, 1)
                if has(b):
                    act.wait_ge(wo_mm, b + 1)
                    if (c - 1) % CH == 0:
                        act.wait_ge(ld["vbo"], 4 * b + 16)
                    nc.scalar.activation(g1[:], ps_b[:], ACT.Gelu_apprx_tanh, bias=vbo[:, 0:1]).then_inc(g1_ready, 1)
                for j in range(FJ):
                    if has(f):
                        act.wait_ge(ff1_mm, 4 * f + j + 1)
                        if j == 0 and (c - 2) % CH == 0:
                            act.wait_ge(ld["vbf1"], 4 * f + 16)
                        nc.scalar.activation(hid[:, j, :], ps_ff[j][:], ACT.Gelu_apprx_tanh,
                                             bias=vbf1[:, j:j + 1]).then_inc(h_ready, 1)
                    if j == 1 and has(d):
                        act.wait_ge(to_fm["D"], d + 1)
                        if (c - 3) % CH == 0:
                            act.wait_ge(ld["vln2"], 4 * d + 16)
                        nc.scalar.activation(xs[(c - 3) % CH][:], ps_d[:], ACT.Identity,
                                             bias=vln2[:, 1:2], scale=vln2[:, 0:1]).then_inc(x_ready, 1)

            slots(act, slot)
            for c in range(CH):
                act.wait_ge(to_fm["F"], c + 1)
                for h in range(HB):
                    b = c * HB + h
                    ev = nc.scalar.activation(half(hf[c], h), half(ps_b, h), ACT.Identity,
                                              bias=mod[:, 3, b:b + 1], scale=m1[:, 1, b:b + 1])
                ev.then_inc(hf_ready, 1)
                act.wait_ge(lg_ready, c + 1)
                nc.scalar.activation(ex[:], lg[:], ACT.Exp).then_inc(ex_ready, 1)
                act.wait_ge(cst_mm, c + 1)
                nc.scalar.activation(cst[c][:], ps_d[:].bitcast(BF16)[0:3 * E, 0:G], ACT.Copy).then_inc(cst_ready, 1)
            gb = [ps_k, ps_q]
            for i in range(CH * U):
                act.wait_ge(gate_mm, i + 1)
                if i >= 2:
                    act.wait_ge(su_ready, i - 1)
                nc.scalar.activation(sg[i % 2][:], gb[i % 2][:], ACT.Silu).then_inc(sg_ready, 1)

        @block.gpsimd
        def _(pool):
            nc.gpsimd.memset(c_half[:], -0.5).then_inc(consts_set, 1)
            nc.gpsimd.memset(c_eps[:], EPS_Z).then_inc(consts_set, 1)
            nc.gpsimd.memset(c_lneps[:], math.log(EPS_Z)).then_inc(consts_set, 1)
            pool.wait_ge(consts_set, 3)

            def rstd(k, n):
                pool.wait_ge(var_ready[k], n + 1)
                nc.gpsimd.tensor_tensor(rs[k][:], ve[k][:], c_half[:], ALU.pow).then_inc(rstd_ready[k], 1)

            for c in range(CH):
                rstd("I", c)

            def slot(s, c, l):
                b, d = s - 1, s - 3
                if has(d):
                    pool.wait_ge(g2_ready, d + 1)
                    nc.gpsimd.tensor_tensor(y2[:], g2[:], x2[(c - 3) % CH][:], ALU.add).then_inc(y2_ready, 1)
                    rstd("D", d)
                if has(b):
                    pool.wait_ge(g1_ready, b + 1)
                    nc.gpsimd.tensor_tensor(y1[:], g1[:], xs[(c - 1) % CH][:], ALU.add).then_inc(y1_ready, 1)
                    rstd("B", b)

            slots(pool, slot)
            for c in range(CH):
                rstd("F", c)

        @block.vector
        def _(dve):
            def stats(k, n, src, eps):
                for j in range(T):
                    bn = nc.vector.bn_stats(st[k][:, j, :], src[:, j, :])
                bn.then_inc(bn_done[k], 1)
                dve.wait_ge(bn_done[k], n + 1)
                s_even, s_odd = st[k][:, :, 1:3], st[k][:, :, 4:6]
                nc.vector.tensor_tensor(dif[k][:], s_even[:, :, 0], s_odd[:, :, 0], ALU.subtract)
                nc.vector.tensor_tensor(mn[k][:], s_even[:, :, 0], s_odd[:, :, 0], ALU.add)
                nc.vector.scalar_tensor_tensor(out=sq[k][:], in0=s_even[:, :, 1], scalar=D * eps, in1=s_odd[:, :, 1],
                                               op0=ALU.add, op1=ALU.add).then_inc(agg_done[k], 1)
                dve.wait_ge(agg_done[k], 2 * n + 1)
                nc.vector.scalar_tensor_tensor(out=dif2[k][:], in0=dif[k][:], scalar=0.25, in1=dif[k][:],
                                               op0=ALU.mult, op1=ALU.mult)
                nc.vector.tensor_scalar(mean[k][:], mn[k][:], 0.5, None, ALU.mult).then_inc(agg_done[k], 1)
                dve.wait_ge(agg_done[k], 2 * n + 2)
                nc.vector.scalar_tensor_tensor(out=ve[k][:], in0=sq[k][:], scalar=1.0 / D, in1=dif2[k][:],
                                               op0=ALU.mult, op1=ALU.add).then_inc(var_ready[k], 1)

            def normalize(k, n, src):
                dve.wait_ge(rstd_ready[k], n + 1)
                for j in range(T):
                    ap = nc.vector.tensor_scalar(xh[k][:, j, :], src[:, j, :], mean[k][:, j:j + 1], rs[k][:, j:j + 1],
                                                 ALU.subtract, ALU.mult)
                ap.then_inc(normed[k], 1)

            def tiles(ps):
                return ps[:].rearrange("p (t d) -> p t d", t=T)

            dve.wait_ge(mod_mm, 1)
            nc.vector.tensor_copy(mod[:].rearrange("p m b -> p (m b)"), ps_y[:, 0:6 * NB]).then_inc(mod_copied, 1)
            dve.wait_ge(mod_copied, 1)
            for i, (cc, gg) in enumerate(((1, 2), (4, 5))):
                nc.vector.tensor_scalar(m1[:, i, :], mod[:, cc, :], 1.0, None, ALU.add).then_inc(ga_parts, 1)
                nc.vector.tensor_scalar(gsg[:, i, :], mod[:, gg, :], 0.0, 2.0, ALU.is_ge, ALU.mult).then_inc(ga_parts, 1)
                nc.vector.scalar_tensor_tensor(out=gab[:, i, :], in0=mod[:, gg, :], scalar=-1.0, in1=mod[:, gg, :],
                                               op0=ALU.mult, op1=ALU.max).then_inc(ga_parts, 1)
            dve.wait_ge(ga_parts, 6)
            nc.vector.tensor_scalar(gab[:], gab[:], 0.25, None, ALU.max).then_inc(ga_parts, 1)
            dve.wait_ge(ga_parts, 7)
            nc.vector.scalar_tensor_tensor(out=gt[:], in0=gsg[:], scalar=-1.0, in1=gab[:],
                                           op0=ALU.add, op1=ALU.mult).then_inc(mod_done, 1)
            for c in range(CH):
                dve.wait_ge(ld["x0"][c], 16)
                stats("I", c, x0[:, c], EPS_MOD)
                if c:
                    dve.wait_ge(to_fm["I"], c)
                normalize("I", c, x0[:, c])

            def slot(s, c, l):
                a, b, d = s, s - 1, s - 3
                if has(a):
                    if c == 0:
                        dve.wait_ge(ld["va"], 16 * l + 16)
                    dve.wait_ge(ek_ready, a + 1)
                    nc.vector.tensor_scalar(mk[:], ek[:], 1.0, -1.0, ALU.min, ALU.add).then_inc(mk_ready, 1)
                    dve.wait_ge(mk_ready, a + 1)
                    nc.vector.scalar_tensor_tensor(out=rk_elu[:], in0=ps_k[:], scalar=va[:, 0:1], in1=mk[:],
                                                   op0=ALU.add, op1=ALU.max).then_inc(elu_k, 1)
                    dve.wait_ge(eq_ready, a + 1)
                    nc.vector.tensor_scalar(mq[:], eq[:], 1.0, -1.0, ALU.min, ALU.add).then_inc(mq_ready, 1)
                    dve.wait_ge(elu_k, a + 1)
                    for h in range(HB):
                        kh = nc.vector.tensor_scalar(half(kk, h), half(rk_elu, h), 1.0, None, ALU.add, ALU.add,
                                                     accum_out=ksum[:, h:h + 1])
                    kh.then_inc(k_ready, 1)
                    dve.wait_ge(mq_ready, a + 1)
                    nc.vector.scalar_tensor_tensor(out=rq_elu[:], in0=ps_q[:], scalar=va[:, 1:2], in1=mq[:],
                                                   op0=ALU.add, op1=ALU.max).then_inc(elu_q, 1)
                    dve.wait_ge(k_ready, a + 1)
                    nc.vector.tensor_scalar(kpos[:], ksum[:], 1e-30, None, ALU.max).then_inc(kpos_ready, 1)
                    dve.wait_ge(elu_q, a + 1)
                    nc.vector.tensor_scalar(qq[:], rq_elu[:], 1.0, None, ALU.add).then_inc(q_ready, 1)
                    dve.wait_ge(v_mm, a + 1)
                    for h in range(HB):
                        kv = nc.vector.scalar_tensor_tensor(out=half(kv_full, h), in0=half(ps_v, h), scalar=va[:, 2:3],
                                                            in1=half(kk, h), op0=ALU.add, op1=ALU.mult,
                                                            accum_out=kvsum[:, h:h + 1])
                    kv.then_inc(kv_ready, 1)
                    dve.wait_ge(kpos_ready, a + 1)
                    nc.vector.reciprocal(rk[:], kpos[:]).then_inc(rk_ready, 1)
                    dve.wait_ge(kv_ready, a + 1)
                    dve.wait_ge(rk_ready, a + 1)
                    nc.vector.tensor_tensor(ck[:], kvsum[:], rk[:], ALU.mult).then_inc(ck_ready, 1)
                    dve.wait_ge(ck_ready, a + 1)
                    nc.vector.tensor_scalar(nck[:], ck[:], -1.0, None, ALU.mult).then_inc(nck_ready, 1)
                if has(d):
                    dve.wait_ge(to_tm["D"], d + 1)
                    stats("D", d, tiles(ps_d), EPS_LN)
                if has(a):
                    dve.wait_ge(nck_ready, a + 1)
                    dve.wait_ge(dd_ready, a + 1)
                    for h in range(HB):
                        vv = nc.vector.tensor_scalar(half(vt[c], h), half(dd, h), nck[:, h:h + 1], ck[:, h:h + 1],
                                                     ALU.mult, ALU.add)
                    vv.then_inc(v_ready, 1)
                if has(d):
                    normalize("D", d, tiles(ps_d))
                if has(b):
                    dve.wait_ge(to_tm["B"], b + 1)
                    stats("B", b, tiles(ps_b), EPS_LN)
                    normalize("B", b, tiles(ps_b))

            slots(dve, slot)

            def step(n, op):
                op.then_inc(rt, 1)
                dve.wait_ge(rt, n)

            dve.wait_ge(ld["moe"], MOE_LOADS)
            nc.vector.tensor_copy(sel[:], sel32[:]).then_inc(moe_consts, 1)
            nc.vector.tensor_copy(identb[:], ident[:]).then_inc(moe_consts, 1)
            STEPS = 13
            for c in range(CH):
                dve.wait_ge(x_ready, NI + c + 1)
                for h in range(HB):
                    b = c * HB + h
                    z = nc.vector.tensor_scalar(half(zf, h), half(xs[c], h), gt[:, 0, b:b + 1], None, ALU.mult)
                z.then_inc(zf_ready, 1)
                dve.wait_ge(to_tm["F"], c + 1)
                nc.vector.tensor_tensor(x0[:, c], tiles(ps_b), x0[:, c], ALU.add).then_inc(x_new, 1)
                dve.wait_ge(x_new, c + 1)
                stats("F", c, x0[:, c], EPS_MOD)
                normalize("F", c, x0[:, c])
                dve.wait_ge(score_mm, c + 1)
                n = STEPS * c
                sc3 = ps_d[:, 0:T * E].rearrange("p (t e) -> p t e", t=T)
                nc.vector.tensor_reduce(mx[:], sc3, AX_X, ALU.max).then_inc(mx_ready, 1)
                dve.wait_ge(mx_ready, c + 1)
                nc.vector.tensor_tensor(lg[:], sc3, mx[:].unsqueeze(2).to_broadcast([P, T, E]),
                                        ALU.subtract).then_inc(lg_ready, 1)
                dve.wait_ge(lg_ready, c + 1)
                own = lg[:].unsqueeze(3).to_broadcast([P, T, E, E])
                other = lg[:].unsqueeze(2).to_broadcast([P, T, E, E])
                low = lower[:].rearrange("p (a b) -> p a b", a=E).unsqueeze(1).to_broadcast([P, T, E, E])

                def v4(t):
                    return t[:].rearrange("p t (a b) -> p t a b", a=E)
                step(n + 1, nc.vector.tensor_tensor(v4(cmp_gt), other, own, ALU.is_gt))
                step(n + 2, nc.vector.tensor_tensor(v4(cmp_eq), other, own, ALU.is_equal))
                step(n + 3, nc.vector.tensor_tensor(v4(cmp_lo), v4(cmp_eq), low, ALU.mult))
                step(n + 4, nc.vector.tensor_tensor(cmp_all[:], cmp_gt[:], cmp_lo[:], ALU.add))
                step(n + 5, nc.vector.tensor_reduce(rank[:], v4(cmp_all), AX_X, ALU.add))
                dve.wait_ge(ex_ready, c + 1)
                step(n + 6, nc.vector.tensor_reduce(sm[:], ex[:], AX_X, ALU.add))
                step(n + 7, nc.vector.reciprocal(rsm[:], sm[:]))
                step(n + 8, nc.vector.scalar_tensor_tensor(out=comb[:], in0=rank[:], scalar=1.5, in1=ex[:],
                                                           op0=ALU.is_lt, op1=ALU.mult))
                step(n + 9, nc.vector.tensor_tensor(comb2[:], comb[:], rsm[:].unsqueeze(2).to_broadcast([P, T, E]),
                                                    ALU.mult))
                if c:
                    dve.wait_ge(cst_mm, c)
                step(n + 10, nc.vector.tensor_copy(cs[:, :, 0, :], comb2[:]))
                step(n + 11, nc.vector.tensor_tensor(res1[:], comb2[:], cs[:, :, 0, :], ALU.subtract))
                step(n + 12, nc.vector.tensor_copy(cs[:, :, 1, :], res1[:]))
                step(n + 13, nc.vector.tensor_tensor(res2[:], res1[:], cs[:, :, 1, :], ALU.subtract))
                nc.vector.tensor_copy(cs[:, :, 2, :], res2[:]).then_inc(cs_ready, 1)

            def finish(c):
                dve.wait_ge(out_tm, c + 1)
                if c >= 2:
                    dve.wait_ge(stored[c % 2], 16 * (c // 2))
                nc.vector.tensor_tensor(ot[c % 2][:], tiles(ps_b), x0[:, c], ALU.add).then_inc(ot_ready, 1)

            ub = [ps_v, ps_f0]
            for i in range(CH * U):
                c, u = divmod(i, U)
                dve.wait_ge(sg_ready, i + 1)
                dve.wait_ge(up_mm, i + 1)
                if i >= 2:
                    dve.wait_ge(down_mm, i - 1)
                if u < E:
                    nc.vector.tensor_tensor(su[i % 2][:], ub[i % 2][:], sg[i % 2][:], ALU.mult).then_inc(su_ready, 1)
                    dve.wait_ge(su_ready, i + 1)
                    dve.wait_ge(bc_mm, routed(i) + 1)
                    nc.vector.tensor_tensor(sc[i % 2][:], ps_f1[:], su[i % 2][:], ALU.mult).then_inc(sc_ready, 1)
                else:
                    nc.vector.tensor_tensor(sc[i % 2][:], ub[i % 2][:], sg[i % 2][:], ALU.mult).then_inc(su_ready, 1)
                if u == 2 and c:
                    finish(c - 1)
                if u == U - 1:
                    dve.wait_ge(down_mm, i + 1)
                    for h in range(HB):
                        b = c * HB + h
                        nc.vector.tensor_scalar(half(yf, h), half(ps_y, h), gt[:, 1, b:b + 1], None,
                                                ALU.mult).then_inc(yf_ready, 1)
            finish(CH - 1)


def kernel(**inputs):
    import numpy as np
    import concourse.bacc as bacc
    from concourse.bass_utils import run_bass_kernel_spmd

    def w(name):
        return np.asarray(inputs[name])

    def stack(*names):
        return np.ascontiguousarray(np.stack([w(n) for n in names], axis=-1))

    select = np.zeros((3, E, E, P), np.float32)
    for e in range(E):
        select[:, e, e, :] = 1.0
    lower = np.broadcast_to(np.tril(np.ones((E, E), np.float32), -1).reshape(1, E * E), (P, E * E))
    sg = w("L0_ffn_shared_gate_w").reshape(D, 2, P).transpose(0, 1, 2)
    su = w("L0_ffn_shared_up_w").reshape(D, 2, P)
    sd = w("L0_ffn_shared_down_w").reshape(2, P, D).transpose(1, 0, 2)
    gates = np.concatenate([w("L0_ffn_gate_w").transpose(1, 0, 2), sg], axis=1)
    ups = np.concatenate([w("L0_ffn_up_w").transpose(1, 0, 2), su], axis=1)
    downs = np.concatenate([w("L0_ffn_down_w").transpose(1, 0, 2), sd], axis=1)
    arrays = {
        "x": w("L0_attn_x").reshape(NB * L, D),
        "w_qkv": np.concatenate([w("L0_attn_Wk"), w("L0_attn_Wq"), w("L0_attn_Wv")], axis=2),
        "w_o": w("L0_attn_Wo"),
        "w_f1": w("L0_attn_Wf1"),
        "w_f2": w("L0_attn_Wf2").reshape(LAYERS, FJ, P, D).transpose(0, 2, 1, 3),
        "v_a": stack("L0_attn_bk", "L0_attn_bq", "L0_attn_bv"),
        "v_bo": stack("L0_attn_bo"),
        "v_ln1": stack("L0_attn_ln1_s", "L0_attn_ln1_b"),
        "v_bf1": w("L0_attn_bf1").reshape(LAYERS, FJ, P).transpose(0, 2, 1),
        "v_bf2": stack("L0_attn_bf2"),
        "v_ln2": stack("L0_attn_ln2_s", "L0_attn_ln2_b"),
        "c_t": w("L0_c").T,
        "w_mod": w("L0_wmod"),
        "w_router": w("L0_ffn_router_w"),
        "w_unit": np.stack([gates, ups, downs], axis=2),
        "ident": np.eye(P, dtype=np.float32),
        "select": select.reshape(3 * E, E * P),
        "lower": lower,
    }
    nc = bacc.Bacc("TRN2", target_bir_lowering=False, num_devices=1)
    arrays = {f"in_{k}": np.ascontiguousarray(a) for k, a in arrays.items()}
    args = [nc.dram_tensor(k, a.shape, mybir.dt.from_np(a.dtype), kind="ExternalInput").ap() for k, a in arrays.items()]
    result = nc.dram_tensor("out_0", (NB * L, D), F32, kind="ExternalOutput").ap()
    adaln_block(nc, *args, result)
    r = run_bass_kernel_spmd(nc, [arrays], core_ids=[0])
    return r.results[0]["out_0"].reshape(NB, L, D)
```

```python
import math
from contextlib import ExitStack

import concourse.bass as bass
from concourse import mybir

ALU = mybir.AluOpType
ACT = mybir.ActivationFunctionType
F32 = mybir.dt.float32
BF16 = mybir.dt.bfloat16
AX_X = mybir.AxisListType.X

P = 128
NB, L, D = 8, 256, 128
LAYERS, F = 8, 512
E = 8
G = 512
CH = NB * L // G
HB = G // L
T = G // P
FJ = F // P
NI = LAYERS * CH
SHARED = 2
U = SHARED + E
EPS_LN, EPS_Z, EPS_MOD = 1e-6, 1e-6, 1e-5
LN_SET = "natural_log_exp_and_others"


def adaln_block(nc, x, w_qkv, w_o, w_f1, w_f2, v_a, v_bo, v_ln1, v_bf1, v_bf2, v_ln2, c_t, w_mod,
                w_router, w_unit, ident_in, select_in, lower_in, out):
    with ExitStack() as ctx:
        def sb(name, shape, dt=F32):
            return ctx.enter_context(nc.sbuf_tensor(name, shape, dt))

        def sem(name):
            return ctx.enter_context(nc.semaphore(name))

        ident = sb("ident", [P, P])
        wqkv = sb("wqkv", [P, 3 * P])
        wo = sb("wo", [P, P])
        wf1 = sb("wf1", [P, F])
        wf2 = sb("wf2", [P, FJ, P])
        va = sb("va", [P, 3])
        vbo = sb("vbo", [P, 1])
        vln1 = sb("vln1", [P, 2])
        vbf1 = sb("vbf1", [P, FJ])
        vbf2 = sb("vbf2", [P, 1])
        vln2 = sb("vln2", [P, 2])
        x0 = sb("x0", [P, CH, T, D])
        xs = [sb(f"xs{c}", [P, G]) for c in range(CH)]
        x2 = [sb(f"x2_{c}", [P, G]) for c in range(CH)]
        vt = [sb(f"vt{c}", [P, G]) for c in range(CH)]
        ek, eq = sb("ek", [P, G]), sb("eq", [P, G])
        mk, mq = sb("mk", [P, G]), sb("mq", [P, G])
        kk, qq, kv_full = sb("kk", [P, G]), sb("qq", [P, G]), sb("kv_full", [P, G])
        lden, dd = sb("lden", [P, G]), sb("dd", [P, G])
        rk_elu, rq_elu, kpos = sb("elu_k_fm", [P, G]), sb("elu_q_fm", [P, G]), sb("kpos", [P, HB])
        ksum, kvsum, rk = sb("ksum", [P, HB]), sb("kvsum", [P, HB]), sb("rk", [P, HB])
        ck, nck = sb("ck", [P, HB]), sb("nck", [P, HB])
        g1, y1, g2, y2 = sb("g1", [P, G]), sb("y1", [P, G]), sb("g2", [P, G]), sb("y2", [P, G])
        hid = sb("hid", [P, FJ, G])
        xh = {k: sb(f"xh{k}", [P, T, D]) for k in "BDF"}
        rows = ["I0", "I1", "I2", "I3", "B", "D", "F0", "F1"]
        st = {k: sb(f"st{k}", [P, T, 6]) for k in rows}
        dif, mn, sq, dif2, mean = ({k: sb(f"{name}{k}", [P, T]) for k in rows}
                                   for name in ("dif", "mn", "sq", "dif2", "mean"))
        ve = {k: sb(f"ve{k}", [P, T]) for k in rows}
        rs = {k: sb(f"rs{k}", [P, T]) for k in rows}
        ones = sb("ones", [P, G])
        c_eps, c_lneps, c_half = sb("c_eps", [P, 1]), sb("c_lneps", [P, 1]), sb("c_half", [P, T])
        ct, sct = sb("ct", [P, NB]), sb("sct", [P, NB])
        wmod = sb("wmod", [P, 6 * D])
        mod = sb("mod", [P, 6, NB])
        m1 = sb("m1", [P, 2, NB])
        gt = sb("gt", [P, 2, NB])
        gsg, gab = sb("gsg", [P, 2, NB]), sb("gab", [P, 2, NB])
        wr = sb("wr", [P, E])
        wu = sb("wu", [P, U, 3, P])
        sel32, sel = sb("sel32", [3 * E, E * P]), sb("sel", [3 * E, E * P], BF16)
        lower = sb("lower", [P, E * E])
        zf = sb("zf", [P, G])
        hf = [sb(f"hf{c}", [P, G]) for c in range(CH)]
        mx, lg, ex = sb("mx", [P, T]), sb("lg", [P, T, E]), sb("ex", [P, T, E])
        sm, rsm = sb("sm", [P, T]), sb("rsm", [P, T])
        cmp_gt, cmp_eq = sb("cmp_gt", [P, T, E * E]), sb("cmp_eq", [P, T, E * E])
        cmp_lo, cmp_all = sb("cmp_lo", [P, T, E * E]), sb("cmp_all", [P, T, E * E])
        rank, comb, comb2 = sb("rank", [P, T, E]), sb("comb", [P, T, E]), sb("comb2", [P, T, E])
        res1, res2 = sb("res1", [P, T, E]), sb("res2", [P, T, E])
        cs = sb("cs", [P, T, 3, E], BF16)
        identb = sb("identb", [P, P], BF16)
        cst = [sb(f"cst{c}", [3 * E, G], BF16) for c in range(CH)]
        sg = [sb(f"sg{i}", [P, G]) for i in range(2)]
        su = [sb(f"su{i}", [P, G]) for i in range(2)]
        sc = [sb(f"sc{i}", [P, G]) for i in range(2)]
        yf = sb("yf", [P, G])
        ot = [sb(f"ot{i}", [P, T, D]) for i in range(2)]

        bank = [ctx.enter_context(nc.psum_tensor(f"bank{i}", [P, G], F32)) for i in range(8)]
        ps_k, ps_q, ps_v, ps_f0, ps_f1, ps_b, ps_d, ps_y = bank
        ps_ff = [ps_f0, ps_f1, ps_y, ps_k]

        gate_bank, up_bank = [ps_k, ps_f1], [ps_b, ps_f0]

        ld = {k: sem(f"ld_{k}") for k in ("const", "mod", "moe", "wqkv", "va", "wo", "vbo", "vln1",
                                          "wf1", "vbf1", "wf2", "vbf2", "vln2")}
        ld["x0"] = [sem(f"ld_x0_{c}") for c in range(CH)]
        consts_set = sem("consts_set")
        silu_c, mod_mm, mod_copied, mod_done = sem("silu_c"), sem("mod_mm"), sem("mod_copied"), sem("mod_done")
        ga_parts = sem("ga_parts")
        k_mm, q_mm, v_mm = sem("k_mm"), sem("q_mm"), sem("v_mm")
        ek_ready, eq_ready = sem("ek_ready"), sem("eq_ready")
        elu_k, elu_q, kpos_ready = sem("elu_k"), sem("elu_q"), sem("kpos_ready")
        mk_ready, k_ready, mq_ready, q_ready = sem("mk_ready"), sem("k_ready"), sem("mq_ready"), sem("q_ready")
        rk_ready, kv_ready, ck_ready, nck_ready = sem("rk_ready"), sem("kv_ready"), sem("ck_ready"), sem("nck_ready")
        lden_ready, dd_ready, v_ready = sem("lden_ready"), sem("dd_ready"), sem("v_ready")
        wo_mm, g1_ready, y1_ready = sem("wo_mm"), sem("g1_ready"), sem("y1_ready")
        ff1_mm, h_ready, ff2_mm, g2_ready, y2_ready = (sem("ff1_mm"), sem("h_ready"), sem("ff2_mm"),
                                                       sem("g2_ready"), sem("y2_ready"))
        x2_ready, x_ready = sem("x2_ready"), sem("x_ready")
        to_tm = {k: sem(f"to_tm{k}") for k in "BDF"}
        bn_done = {k: sem(f"bn_done{k}") for k in "IBDF"}
        agg_done = {k: sem(f"agg_done{k}") for k in "IBDF"}
        var_ready = {k: sem(f"var_ready{k}") for k in "IBDF"}
        rstd_ready = {k: sem(f"rstd_ready{k}") for k in "IBDF"}
        normed = {k: sem(f"normed{k}") for k in "IBDF"}
        to_fm = {k: sem(f"to_fm{k}") for k in "IBDF"}
        zf_ready, x_new, hf_ready = sem("zf_ready"), sem("x_new"), sem("hf_ready")
        moe_consts, score_mm, lg_ready, ex_ready = (sem("moe_consts"), sem("score_mm"), sem("lg_ready"), sem("ex_ready"))
        rt = sem("rt")
        cs_ready, cst_mm, cst_ready = sem("cs_ready"), sem("cst_mm"), sem("cst_ready")
        gate_mm, up_mm, bc_mm, down_mm = sem("gate_mm"), sem("up_mm"), sem("bc_mm"), sem("down_mm")
        sg_ready, su_ready, sc_ready = sem("sg_ready"), sem("su_ready"), sem("sc_ready")
        yf_ready, out_tm, ot_ready, stored = sem("yf_ready"), sem("out_tm"), sem("ot_ready"), [sem(f"stored{i}") for i in range(2)]

        x_rows = x.rearrange("(c h p j) d -> p c h j d", c=CH, h=HB, p=P)
        out_rows = out.rearrange("(c h p j) d -> p c h j d", c=CH, h=HB, p=P)

        def buf(k, n):
            return f"F{n % 2}" if k == "F" else f"I{n}" if k == "I" else k

        def rows_of(k, n):
            return hf[n][:].rearrange("p (t d) -> p t d", t=T) if k == "I" else xh[k][:]

        def half(ap, h):
            return ap[:, h * L:(h + 1) * L]

        def has(n):
            return not isinstance(n, int) or 0 <= n < NI

        def wait(eng, s, value):
            if not isinstance(value, int) or value > 0:
                eng.wait_ge(s, value)

        def routed(i):
            return i // U * E + max(i % U - SHARED, 0)

        def slots(eng, one_slot, between=None):
            if between:
                one_slot(0, 0, 0, between)
            else:
                one_slot(0, 0, 0)
            for s in range(1, CH - 1):
                one_slot(s, s % CH, s // CH)
            with eng.Fori(0, LAYERS - 1) as i:
                for j in range(CH):
                    s = CH - 1 + j
                    one_slot(i * CH + s, s % CH, i + s // CH)
            one_slot(NI - 1, CH - 1, LAYERS - 1)

        block = ctx.enter_context(nc.Block())

        @block.sync
        def _(sp):
            for c in range(CH):
                sp.dma_start(x0[:, c, :, :].rearrange("p (h j) d -> p h j d", h=HB), x_rows[:, c]).then_inc(ld["x0"][c], 16)
                if c == 0:
                    sp.dma_start(ident[:], ident_in).then_inc(ld["const"], 16)

            def layer_loads(l, first):
                if not first:
                    sp.wait_ge(v_mm, CH * l)
                    sp.dma_start(wqkv[:], w_qkv[l]).then_inc(ld["wqkv"], 16)
                    sp.wait_ge(kv_ready, CH * l)
                    sp.wait_ge(elu_q, CH * l)
                    sp.dma_start(va[:], v_a[l]).then_inc(ld["va"], 16)
                if not first:
                    sp.wait_ge(wo_mm, CH * l)
                sp.dma_start(wo[:], w_o[l]).then_inc(ld["wo"], 16)
                if not first:
                    sp.wait_ge(g1_ready, CH * l)
                sp.dma_start(vbo[:], v_bo[l]).then_inc(ld["vbo"], 16)
                if not first:
                    sp.wait_ge(x2_ready, HB * CH * l)
                sp.dma_start(vln1[:], v_ln1[l]).then_inc(ld["vln1"], 16)
                if not first:
                    sp.wait_ge(ff1_mm, FJ * CH * l)
                sp.dma_start(wf1[:], w_f1[l]).then_inc(ld["wf1"], 16)
                if not first:
                    sp.wait_ge(h_ready, FJ * CH * l)
                sp.dma_start(vbf1[:], v_bf1[l]).then_inc(ld["vbf1"], 16)
                if not first:
                    sp.wait_ge(ff2_mm, CH * l)
                sp.dma_start(wf2[:], w_f2[l]).then_inc(ld["wf2"], 16)
                if not first:
                    sp.wait_ge(g2_ready, CH * l)
                sp.dma_start(vbf2[:], v_bf2[l]).then_inc(ld["vbf2"], 16)
                if not first:
                    sp.wait_ge(x_ready, CH * l + CH)
                sp.dma_start(vln2[:], v_ln2[l]).then_inc(ld["vln2"], 16)

            layer_loads(0, True)
            sp.dma_start(wr[:], w_router).then_inc(ld["moe"], 16)
            sp.dma_start(sel32[:], select_in).then_inc(ld["moe"], 16)
            sp.dma_start(lower[:], lower_in).then_inc(ld["moe"], 16)
            for u in range(U):
                sp.dma_start(wu[:, u], w_unit[:, u]).then_inc(ld["moe"], 16)
            with sp.Fori(1, LAYERS) as l:
                layer_loads(l, False)
            for c in range(CH):
                sp.wait_ge(ot_ready, c + 1)
                sp.dma_start(out_rows[:, c], ot[c % 2][:, :, :].rearrange("p (h j) d -> p h j d", h=HB)).then_inc(stored[c % 2], 16)
            for i in range(2):
                sp.wait_ge(stored[i], 16 * CH // 2)

        MOE_LOADS = 16 * (3 + U)

        @block.tensor
        def _(pe):
            def transposes(out_bank, src, done):
                for j in range(T):
                    t = src[:, j, :] if len(src.shape) == 3 else src[:, j * P:(j + 1) * P]
                    mm = nc.tensor.transpose(out_bank[:, j * P:(j + 1) * P], t, ident[:])
                mm.then_inc(done, 1)

            pe.wait_ge(ld["const"], 16)
            pe.wait_ge(ld["mod"], 32)
            pe.wait_ge(silu_c, 1)
            for m in range(6):
                mm = nc.tensor.matmul(ps_y[:, m * NB:(m + 1) * NB], wmod[:, m * D:(m + 1) * D], sct[:],
                                      start=True, stop=True)
            mm.then_inc(mod_mm, 1)
            def first_to_fm(c):
                pe.wait_ge(normed["I"], c + 1)
                transposes([ps_f0, ps_f1, ps_b, ps_d][c], rows_of("I", c), to_fm["I"])

            def rest_to_fm():
                for c in range(1, CH):
                    first_to_fm(c)

            first_to_fm(0)

            def slot(s, c, l, between=None):
                a, b, f, d = s, s - 1, s - 2, s - 3
                if has(a):
                    pe.wait_ge(x_ready, a + 1)
                    if c == 0:
                        pe.wait_ge(ld["wqkv"], 4 * a + 16)
                    if has(a - 3):
                        pe.wait_ge(h_ready, 4 * (a - 3) + 4)
                    elif has(a - 1):
                        pe.wait_ge(elu_k, a)
                    nc.tensor.matmul(ps_k[:], wqkv[:, 0:P], xs[c][:], start=True, stop=True).then_inc(k_mm, 1)
                    if has(a - 1):
                        pe.wait_ge(elu_q, a)
                    nc.tensor.matmul(ps_q[:], wqkv[:, P:2 * P], xs[c][:], start=True, stop=True).then_inc(q_mm, 1)
                    if has(a - 1):
                        pe.wait_ge(kv_ready, a)
                    nc.tensor.matmul(half(ps_v, 0), wqkv[:, 2 * P:3 * P], half(xs[c], 0), start=True, stop=True)
                if has(f):
                    pe.wait_ge(normed["B"], f + 1)
                    transposes(ps_b, xh["B"], to_fm["B"])
                if has(a):
                    nc.tensor.matmul(half(ps_v, 1), wqkv[:, 2 * P:3 * P], half(xs[c], 1),
                                     start=True, stop=True).then_inc(v_mm, 1)
                if has(d):
                    pe.wait_ge(y2_ready, d + 1)
                    pe.wait_ge(x_ready, d + CH)
                    transposes(ps_d, y2, to_tm["D"])
                def ff1(j):
                    if j == 0:
                        wait(pe, g2_ready, f)
                        if isinstance(f, int) and f == 0:
                            pe.wait_ge(mod_copied, 1)
                        if (c - 2) % CH == 0:
                            pe.wait_ge(ld["wf1"], 4 * f + 16)
                    if j == 3:
                        pe.wait_ge(elu_k, a + 1 if has(a) else NI)
                        if not has(a):
                            pe.wait_ge(h_ready, 4 * f)
                    if j == 0:
                        for h in range(HB):
                            pe.wait_ge(x2_ready, HB * f + h + 1)
                            mm = nc.tensor.matmul(half(ps_ff[0], h), wf1[:, 0:P], half(x2[(c - 2) % CH], h),
                                                  start=True, stop=True)
                    else:
                        mm = nc.tensor.matmul(ps_ff[j][:], wf1[:, j * P:(j + 1) * P], x2[(c - 2) % CH][:],
                                              start=True, stop=True)
                    mm.then_inc(ff1_mm, 1)

                def ff2(j):
                    if j == 0 and (c - 2) % CH == 0:
                        pe.wait_ge(ld["wf2"], 4 * f + 16)
                    pe.wait_ge(h_ready, 4 * f + j + 1)
                    mm = nc.tensor.matmul(ps_f0[:], wf2[:, j, :], hid[:, j, :], start=(j == 0), stop=(j == FJ - 1))
                    if j == FJ - 1:
                        mm.then_inc(ff2_mm, 1)

                if has(f):
                    ff1(0)
                    ff1(1)
                    ff1(2)
                if has(b):
                    pe.wait_ge(v_ready, b + 1)
                    if (c - 1) % CH == 0:
                        pe.wait_ge(ld["wo"], 4 * b + 16)
                    wait(pe, x2_ready, HB * b)
                    if isinstance(b, int) and b == 0:
                        pe.wait_ge(x_ready, CH)
                    nc.tensor.matmul(ps_b[:], wo[:], vt[(c - 1) % CH][:], start=True, stop=True).then_inc(wo_mm, 1)
                if has(f):
                    ff2(0)
                    ff1(3)
                if between:
                    between()
                if has(f):
                    ff2(1)
                if has(b):
                    pe.wait_ge(y1_ready, b + 1)
                    transposes(ps_b, y1, to_tm["B"])
                if has(d):
                    pe.wait_ge(normed["D"], d + 1)
                    transposes(ps_d, xh["D"], to_fm["D"])
                if has(f):
                    ff2(2)
                    ff2(3)

            slots(pe, slot, rest_to_fm)

            last = NI - 1

            def zf_to_tm(c):
                pe.wait_ge(zf_ready, c + 1)
                if c == 0:
                    pe.wait_ge(elu_q, NI)
                if c:
                    pe.wait_ge(x_new, c)
                if c >= 2:
                    pe.wait_ge(lg_ready, c - 1)
                transposes(ps_q, zf, to_tm["F"])

            def norm_to_fm(c):
                pe.wait_ge(normed["F"], c + 1)
                pe.wait_ge(kv_ready, NI)
                if c:
                    pe.wait_ge(hf_ready, c)
                if c >= 2:
                    pe.wait_ge(cst_ready, c - 1)
                transposes(ps_v, xh["F"], to_fm["F"])

            def scores(c):
                pe.wait_ge(hf_ready, c + 1)
                pe.wait_ge(x_new, min(c + 2, CH))
                if c:
                    pe.wait_ge(lg_ready, c)
                for j in range(T):
                    mm = nc.tensor.matmul(ps_q[:, j * E:(j + 1) * E], hf[c][:, j * P:(j + 1) * P], wr[:],
                                          start=True, stop=True)
                mm.then_inc(score_mm, 1)

            def weights_to_fm(c):
                pe.wait_ge(cs_ready, c + 1)
                pe.wait_ge(hf_ready, min(c + 2, CH))
                if c:
                    pe.wait_ge(cst_ready, c)
                psb = ps_v[:].bitcast(BF16)
                for j in range(T):
                    mm = nc.tensor.transpose(psb[0:3 * E, j * P:(j + 1) * P],
                                             cs[:, j, :, :].rearrange("p a e -> p (a e)"), identb[:])
                mm.then_inc(cst_mm, 1)

            def down(i):
                c, u = divmod(i, U)
                if u >= SHARED:
                    pe.wait_ge(sc_ready, routed(i) + 1)
                else:
                    pe.wait_ge(su_ready, i + 1)
                if u == 0 and c:
                    pe.wait_ge(yf_ready, HB * c)
                mm = nc.tensor.matmul(ps_y[:], wu[:, u, 2, :], sc[i % 2][:], start=(u == 0), stop=(u == U - 1))
                mm.then_inc(down_mm, 1)

            def result_to_tm(c):
                pe.wait_ge(yf_ready, HB * (c + 1))
                pe.wait_ge(lg_ready, CH)
                if c:
                    pe.wait_ge(ot_ready, c)
                transposes(ps_q, yf, out_tm)

            zf_to_tm(0)
            slot(NI, 0, LAYERS)
            zf_to_tm(1)
            slot(NI + 1, 1, LAYERS, lambda: norm_to_fm(0))
            pe.wait_ge(ld["moe"], MOE_LOADS)
            scores(0)
            pe.wait_ge(h_ready, FJ * NI)
            pe.wait_ge(x2_ready, HB * NI)
            for i in range(CH * U):
                c, u = divmod(i, U)
                if i == 0:
                    zf_to_tm(2)
                if i == 1:
                    pe.wait_ge(y2_ready, NI)
                    pe.wait_ge(x_ready, last + CH)
                    transposes(ps_d, y2, to_tm["D"])
                    norm_to_fm(1)
                if i == 2:
                    pe.wait_ge(moe_consts, 2)
                    weights_to_fm(0)
                if i == 3:
                    scores(1)
                if i == 4:
                    norm_to_fm(2)
                if i == 6:
                    zf_to_tm(3)
                if i == 7:
                    weights_to_fm(1)
                if i == 8:
                    scores(2)
                if i == 9:
                    norm_to_fm(3)
                if i == 10:
                    scores(3)
                if i == 12:
                    weights_to_fm(2)
                if i == 15:
                    weights_to_fm(3)
                if u == 0:
                    pe.wait_ge(hf_ready, c + 1)
                if i == 1:
                    pe.wait_ge(g2_ready, NI)
                if i >= 2:
                    pe.wait_ge(sg_ready, i - 1)
                nc.tensor.matmul(gate_bank[i % 2][:], wu[:, u, 0, :], hf[c][:], start=True, stop=True).then_inc(gate_mm, 1)
                if i >= 2:
                    pe.wait_ge(su_ready, i - 1)
                nc.tensor.matmul(up_bank[i % 2][:], wu[:, u, 1, :], hf[c][:], start=True, stop=True).then_inc(up_mm, 1)
                if i:
                    down(i - 1)
                if i == 2:
                    pe.wait_ge(normed["D"], NI)
                    transposes(ps_d, xh["D"], to_fm["D"])
                    pe.wait_ge(x_ready, NI + CH)
                if u >= SHARED:
                    if u == SHARED:
                        pe.wait_ge(cst_ready, c + 1)
                    if routed(i):
                        pe.wait_ge(sc_ready, routed(i))
                    e = u - SHARED
                    nc.tensor.matmul(ps_d[:], sel[:, e * P:(e + 1) * P], cst[c][:], start=True, stop=True).then_inc(bc_mm, 1)
                if u == 3 and c:
                    result_to_tm(c - 1)
            down(CH * U - 1)
            result_to_tm(CH - 1)

        @block.scalar
        def _(act):
            act.dma_start(ct[:], c_t).then_inc(ld["mod"], 16)
            act.dma_start(wmod[:], w_mod).then_inc(ld["mod"], 16)
            act.dma_start(wqkv[:], w_qkv[0]).then_inc(ld["wqkv"], 16)
            act.dma_start(va[:], v_a[0]).then_inc(ld["va"], 16)
            act.wait_ge(ld["mod"], 32)
            nc.scalar.activation(sct[:], ct[:], ACT.Silu).then_inc(silu_c, 1)
            act.wait_ge(mod_done, 1)
            def first_norm(c):
                act.wait_ge(to_fm["I"], c + 1)
                for h in range(HB):
                    b = c * HB + h
                    ev = nc.scalar.activation(half(xs[c], h), half([ps_f0, ps_f1, ps_b, ps_d][c], h), ACT.Identity,
                                              bias=mod[:, 0, b:b + 1], scale=m1[:, 0, b:b + 1])
                ev.then_inc(x_ready, 1)

            def rest_of_first_norm():
                for c in range(1, CH):
                    first_norm(c)

            first_norm(0)
            act.wait_ge(consts_set, 4)

            def slot(s, c, l, between=None):
                a, b, f, d = s, s - 1, s - 2, s - 3
                if has(d):
                    act.wait_ge(ff2_mm, d + 1)
                    if (c - 3) % CH == 0:
                        act.wait_ge(ld["vbf2"], 4 * d + 16)
                    nc.scalar.activation(g2[:], ps_f0[:], ACT.Gelu_apprx_tanh, bias=vbf2[:, 0:1]).then_inc(g2_ready, 1)
                if has(a) or has(b):
                    nc.scalar.preload_act_table_set(LN_SET)
                if has(b):
                    act.wait_ge(q_ready, b + 1)
                    act.wait_ge(k_ready, b + 1)
                    for h in range(HB):
                        ln = nc.scalar.activation(half(lden, h), half(qq, h), ACT.Ln,
                                                  bias=c_eps[:, 0:1], scale=ksum[:, h:h + 1])
                    ln.then_inc(lden_ready, 1)
                    act.wait_ge(lden_ready, b + 1)
                    nc.scalar.activation(dd[:], lden[:], ACT.Exp, bias=c_lneps[:, 0:1], scale=-1.0).then_inc(dd_ready, 1)
                if has(a):
                    act.wait_ge(k_mm, a + 1)
                    if c == 0:
                        act.wait_ge(ld["va"], 4 * a + 16)
                    nc.scalar.activation(ek[:], ps_k[:], ACT.Exp, bias=va[:, 0:1]).then_inc(ek_ready, 1)
                    act.wait_ge(q_mm, a + 1)
                    nc.scalar.activation(eq[:], ps_q[:], ACT.Exp, bias=va[:, 1:2]).then_inc(eq_ready, 1)
                for j in range(FJ):
                    if has(f):
                        act.wait_ge(ff1_mm, 4 * f + j + 1)
                        if j == 0 and (c - 2) % CH == 0:
                            act.wait_ge(ld["vbf1"], 4 * f + 16)
                        nc.scalar.activation(hid[:, j, :], ps_ff[j][:], ACT.Gelu_apprx_tanh,
                                             bias=vbf1[:, j:j + 1]).then_inc(h_ready, 1)
                    if j == 0 and has(b):
                        act.wait_ge(wo_mm, b + 1)
                        if (c - 1) % CH == 0:
                            act.wait_ge(ld["vbo"], 4 * b + 16)
                        nc.scalar.activation(g1[:], ps_b[:], ACT.Gelu_apprx_tanh, bias=vbo[:, 0:1]).then_inc(g1_ready, 1)
                    if j == 1 and between:
                        between()
                    if j == 3 and has(d):
                        act.wait_ge(to_fm["D"], d + 1)
                        if (c - 3) % CH == 0:
                            act.wait_ge(ld["vln2"], 4 * d + 16)
                        nc.scalar.activation(xs[(c - 3) % CH][:], ps_d[:], ACT.Identity,
                                             bias=vln2[:, 1:2], scale=vln2[:, 0:1]).then_inc(x_ready, 1)

            slots(act, slot, rest_of_first_norm)
            def second_norm(c):
                act.wait_ge(to_fm["F"], c + 1)
                for h in range(HB):
                    b = c * HB + h
                    ev = nc.scalar.activation(half(hf[c], h), half(ps_v, h), ACT.Identity,
                                              bias=mod[:, 3, b:b + 1], scale=m1[:, 1, b:b + 1])
                ev.then_inc(hf_ready, 1)

            def exponentials(c):
                act.wait_ge(lg_ready, c + 1)
                nc.scalar.activation(ex[:], lg[:], ACT.Exp).then_inc(ex_ready, 1)

            def weights(c):
                act.wait_ge(cst_mm, c + 1)
                nc.scalar.activation(cst[c][:], ps_v[:].bitcast(BF16)[0:3 * E, 0:G], ACT.Copy).then_inc(cst_ready, 1)

            slot(NI, 0, LAYERS)
            slot(NI + 1, 1, LAYERS, lambda: second_norm(0))
            act.wait_ge(ff2_mm, NI)
            nc.scalar.activation(g2[:], ps_f0[:], ACT.Gelu_apprx_tanh, bias=vbf2[:, 0:1]).then_inc(g2_ready, 1)
            exponentials(0)
            for i in range(CH * U):
                if i == 1:
                    second_norm(1)
                if i == 2:
                    weights(0)
                if i == 3:
                    act.wait_ge(to_fm["D"], NI)
                    nc.scalar.activation(xs[CH - 1][:], ps_d[:], ACT.Identity,
                                         bias=vln2[:, 1:2], scale=vln2[:, 0:1]).then_inc(x_ready, 1)
                if i == 4:
                    exponentials(1)
                    second_norm(2)
                if i == 7:
                    weights(1)
                if i == 9:
                    exponentials(2)
                    second_norm(3)
                if i == 12:
                    exponentials(3)
                    weights(2)
                if i == 15:
                    weights(3)
                act.wait_ge(gate_mm, i + 1)
                if i >= 2:
                    act.wait_ge(su_ready, i - 1)
                nc.scalar.activation(sg[i % 2][:], gate_bank[i % 2][:], ACT.Silu).then_inc(sg_ready, 1)

        @block.gpsimd
        def _(pool):
            nc.gpsimd.memset(ones[:], 1.0).then_inc(consts_set, 1)
            nc.gpsimd.memset(c_half[:], -0.5).then_inc(consts_set, 1)
            nc.gpsimd.memset(c_eps[:], EPS_Z).then_inc(consts_set, 1)
            nc.gpsimd.memset(c_lneps[:], math.log(EPS_Z)).then_inc(consts_set, 1)
            pool.wait_ge(consts_set, 4)

            def rstd(k, n):
                pool.wait_ge(var_ready[k], n + 1)
                nc.gpsimd.tensor_tensor(rs[buf(k, n)][:], ve[buf(k, n)][:], c_half[:], ALU.pow).then_inc(rstd_ready[k], 1)

            for c in range(CH):
                rstd("I", c)

            def slot(s, c, l):
                a, b, d = s, s - 1, s - 3
                if has(d):
                    pool.wait_ge(g2_ready, d + 1)
                    nc.gpsimd.tensor_tensor(y2[:], g2[:], x2[(c - 3) % CH][:], ALU.add).then_inc(y2_ready, 1)
                    rstd("D", d)
                if has(b):
                    pool.wait_ge(g1_ready, b + 1)
                    nc.gpsimd.tensor_tensor(y1[:], g1[:], xs[(c - 1) % CH][:], ALU.add).then_inc(y1_ready, 1)
                if has(a):
                    pool.wait_ge(elu_q, a + 1)
                    nc.gpsimd.tensor_tensor(qq[:], rq_elu[:], ones[:], ALU.add).then_inc(q_ready, 1)
                if has(b):
                    rstd("B", b)

            slots(pool, slot)
            slot(NI, 0, LAYERS)
            rstd("F", 0)
            slot(NI + 1, 1, LAYERS)
            rstd("F", 1)
            slot(NI + 2, 2, LAYERS)
            rstd("F", 2)
            rstd("F", 3)

        @block.vector
        def _(dve):
            def stats(k, n, src, eps):
                q = buf(k, n)
                for j in range(T):
                    bn = nc.vector.bn_stats(st[q][:, j, :], src[:, j, :])
                bn.then_inc(bn_done[k], 1)
                dve.wait_ge(bn_done[k], n + 1)
                s_even, s_odd = st[q][:, :, 1:3], st[q][:, :, 4:6]
                nc.vector.tensor_tensor(dif[q][:], s_even[:, :, 0], s_odd[:, :, 0], ALU.subtract)
                nc.vector.tensor_tensor(mn[q][:], s_even[:, :, 0], s_odd[:, :, 0], ALU.add)
                nc.vector.scalar_tensor_tensor(out=sq[q][:], in0=s_even[:, :, 1], scalar=D * eps, in1=s_odd[:, :, 1],
                                               op0=ALU.add, op1=ALU.add).then_inc(agg_done[k], 1)
                dve.wait_ge(agg_done[k], 2 * n + 1)
                nc.vector.scalar_tensor_tensor(out=dif2[q][:], in0=dif[q][:], scalar=0.25, in1=dif[q][:],
                                               op0=ALU.mult, op1=ALU.mult)
                nc.vector.tensor_scalar(mean[q][:], mn[q][:], 0.5, None, ALU.mult).then_inc(agg_done[k], 1)
                dve.wait_ge(agg_done[k], 2 * n + 2)
                nc.vector.scalar_tensor_tensor(out=ve[q][:], in0=sq[q][:], scalar=1.0 / D, in1=dif2[q][:],
                                               op0=ALU.mult, op1=ALU.add).then_inc(var_ready[k], 1)

            def normalize(k, n, src):
                q = buf(k, n)
                dve.wait_ge(rstd_ready[k], n + 1)
                for j in range(T):
                    ap = nc.vector.tensor_scalar(rows_of(k, n)[:, j, :], src[:, j, :], mean[q][:, j:j + 1], rs[q][:, j:j + 1],
                                                 ALU.subtract, ALU.mult)
                ap.then_inc(normed[k], 1)

            def tiles(ps):
                return ps[:].rearrange("p (t d) -> p t d", t=T)

            def modulation():
                dve.wait_ge(mod_mm, 1)
                nc.vector.tensor_copy(mod[:].rearrange("p m b -> p (m b)"), ps_y[:, 0:6 * NB]).then_inc(mod_copied, 1)
                dve.wait_ge(mod_copied, 1)
                for i, (cc, gg) in enumerate(((1, 2), (4, 5))):
                    nc.vector.tensor_scalar(m1[:, i, :], mod[:, cc, :], 1.0, None, ALU.add).then_inc(ga_parts, 1)
                    nc.vector.tensor_scalar(gsg[:, i, :], mod[:, gg, :], 0.0, 2.0, ALU.is_ge, ALU.mult).then_inc(ga_parts, 1)
                    nc.vector.scalar_tensor_tensor(out=gab[:, i, :], in0=mod[:, gg, :], scalar=-1.0, in1=mod[:, gg, :],
                                                   op0=ALU.mult, op1=ALU.max).then_inc(ga_parts, 1)
                dve.wait_ge(ga_parts, 6)
                nc.vector.tensor_scalar(gab[:], gab[:], 0.25, None, ALU.max).then_inc(ga_parts, 1)
                dve.wait_ge(ga_parts, 7)
                nc.vector.scalar_tensor_tensor(out=gt[:], in0=gsg[:], scalar=-1.0, in1=gab[:],
                                               op0=ALU.add, op1=ALU.mult).then_inc(mod_done, 1)

            for c in range(CH):
                dve.wait_ge(ld["x0"][c], 16)
                stats("I", c, x0[:, c], EPS_MOD)
                if c:
                    normalize("I", c - 1, x0[:, c - 1])
                if c == 1:
                    modulation()
            normalize("I", CH - 1, x0[:, CH - 1])

            def slot(s, c, l, between=None):
                a, b, f, d = s, s - 1, s - 2, s - 3
                if has(f):
                    dve.wait_ge(to_fm["B"], f + 1)
                    if (c - 2) % CH == 0:
                        dve.wait_ge(ld["vln1"], 4 * f + 16)
                    for h in range(HB):
                        nc.vector.tensor_scalar(half(x2[(c - 2) % CH], h), half(ps_b, h), vln1[:, 0:1], vln1[:, 1:2],
                                                ALU.mult, ALU.add).then_inc(x2_ready, 1)
                if has(d):
                    dve.wait_ge(to_tm["D"], d + 1)
                    stats("D", d, tiles(ps_d), EPS_LN)
                if between:
                    between()
                if has(b):
                    dve.wait_ge(nck_ready, b + 1)
                    dve.wait_ge(dd_ready, b + 1)
                    for h in range(HB):
                        vv = nc.vector.tensor_scalar(half(vt[(c - 1) % CH], h), half(dd, h), nck[:, h:h + 1],
                                                     ck[:, h:h + 1], ALU.mult, ALU.add)
                    vv.then_inc(v_ready, 1)
                if has(a):
                    if c == 0:
                        dve.wait_ge(ld["va"], 16 * l + 16)
                    dve.wait_ge(ek_ready, a + 1)
                    nc.vector.tensor_scalar(mk[:], ek[:], 1.0, -1.0, ALU.min, ALU.add).then_inc(mk_ready, 1)
                    dve.wait_ge(mk_ready, a + 1)
                    nc.vector.scalar_tensor_tensor(out=rk_elu[:], in0=ps_k[:], scalar=va[:, 0:1], in1=mk[:],
                                                   op0=ALU.add, op1=ALU.max).then_inc(elu_k, 1)
                if has(d):
                    normalize("D", d, tiles(ps_d))
                if has(a):
                    dve.wait_ge(eq_ready, a + 1)
                    nc.vector.tensor_scalar(mq[:], eq[:], 1.0, -1.0, ALU.min, ALU.add).then_inc(mq_ready, 1)
                    dve.wait_ge(elu_k, a + 1)
                    for h in range(HB):
                        kh = nc.vector.tensor_scalar(half(kk, h), half(rk_elu, h), 1.0, None, ALU.add, ALU.add,
                                                     accum_out=ksum[:, h:h + 1])
                    kh.then_inc(k_ready, 1)
                    dve.wait_ge(mq_ready, a + 1)
                    nc.vector.scalar_tensor_tensor(out=rq_elu[:], in0=ps_q[:], scalar=va[:, 1:2], in1=mq[:],
                                                   op0=ALU.add, op1=ALU.max).then_inc(elu_q, 1)
                    dve.wait_ge(k_ready, a + 1)
                    nc.vector.tensor_scalar(kpos[:], ksum[:], 1e-30, None, ALU.max).then_inc(kpos_ready, 1)
                if has(b):
                    dve.wait_ge(to_tm["B"], b + 1)
                    stats("B", b, tiles(ps_b), EPS_LN)
                if has(a):
                    dve.wait_ge(v_mm, a + 1)
                    for h in range(HB):
                        kv = nc.vector.scalar_tensor_tensor(out=half(kv_full, h), in0=half(ps_v, h), scalar=va[:, 2:3],
                                                            in1=half(kk, h), op0=ALU.add, op1=ALU.mult,
                                                            accum_out=kvsum[:, h:h + 1])
                    kv.then_inc(kv_ready, 1)
                    dve.wait_ge(kpos_ready, a + 1)
                    nc.vector.reciprocal(rk[:], kpos[:]).then_inc(rk_ready, 1)
                if has(b):
                    normalize("B", b, tiles(ps_b))
                if has(a):
                    dve.wait_ge(kv_ready, a + 1)
                    dve.wait_ge(rk_ready, a + 1)
                    nc.vector.tensor_tensor(ck[:], kvsum[:], rk[:], ALU.mult).then_inc(ck_ready, 1)
                    dve.wait_ge(ck_ready, a + 1)
                    nc.vector.tensor_scalar(nck[:], ck[:], -1.0, None, ALU.mult).then_inc(nck_ready, 1)

            slots(dve, slot)

            STEPS = 12

            def step(n, op):
                op.then_inc(rt, 1)
                dve.wait_ge(rt, n)

            def scaled(c):
                dve.wait_ge(x_ready, NI + c + 1)
                for h in range(HB):
                    b = c * HB + h
                    z = nc.vector.tensor_scalar(half(zf, h), half(xs[c], h), gt[:, 0, b:b + 1], None, ALU.mult)
                z.then_inc(zf_ready, 1)

            def residual(c):
                dve.wait_ge(to_tm["F"], c + 1)
                nc.vector.tensor_tensor(x0[:, c], tiles(ps_q), x0[:, c], ALU.add).then_inc(x_new, 1)
                dve.wait_ge(x_new, c + 1)
                stats("F", c, x0[:, c], EPS_MOD)

            def second_norm(c):
                if c:
                    dve.wait_ge(to_fm["F"], c)
                normalize("F", c, x0[:, c])

            own = lg[:].unsqueeze(3).to_broadcast([P, T, E, E])
            other = lg[:].unsqueeze(2).to_broadcast([P, T, E, E])
            low = lower[:].rearrange("p (a b) -> p a b", a=E).unsqueeze(1).to_broadcast([P, T, E, E])

            def v4(t):
                return t[:].rearrange("p t (a b) -> p t a b", a=E)

            def route_scores(c):
                n = STEPS * c
                dve.wait_ge(score_mm, c + 1)
                score = ps_q[:, 0:T * E].rearrange("p (t e) -> p t e", t=T)
                step(n + 1, nc.vector.tensor_reduce(mx[:], score, AX_X, ALU.max))
                nc.vector.tensor_tensor(lg[:], score, mx[:].unsqueeze(2).to_broadcast([P, T, E]),
                                        ALU.subtract).then_inc(lg_ready, 1)
                dve.wait_ge(lg_ready, c + 1)
                nc.vector.tensor_tensor(v4(cmp_gt), other, own, ALU.is_gt)
                step(n + 2, nc.vector.tensor_tensor(v4(cmp_eq), other, own, ALU.is_equal))

            def route_ranks(c):
                n = STEPS * c
                step(n + 3, nc.vector.tensor_tensor(v4(cmp_lo), v4(cmp_eq), low, ALU.mult))
                step(n + 4, nc.vector.tensor_tensor(cmp_all[:], cmp_gt[:], cmp_lo[:], ALU.add))
                step(n + 5, nc.vector.tensor_reduce(rank[:], v4(cmp_all), AX_X, ALU.add))
                dve.wait_ge(ex_ready, c + 1)
                step(n + 6, nc.vector.tensor_reduce(sm[:], ex[:], AX_X, ALU.add))
                nc.vector.reciprocal(rsm[:], sm[:])
                step(n + 7, nc.vector.scalar_tensor_tensor(out=comb[:], in0=rank[:], scalar=1.5, in1=ex[:],
                                                           op0=ALU.is_lt, op1=ALU.mult))

            def route_weights(c):
                n = STEPS * c
                step(n + 8, nc.vector.tensor_tensor(comb2[:], comb[:], rsm[:].unsqueeze(2).to_broadcast([P, T, E]),
                                                    ALU.mult))
                if c:
                    dve.wait_ge(cst_mm, c)
                step(n + 9, nc.vector.tensor_copy(cs[:, :, 0, :], comb2[:]))
                step(n + 10, nc.vector.tensor_tensor(res1[:], comb2[:], cs[:, :, 0, :], ALU.subtract))
                step(n + 11, nc.vector.tensor_copy(cs[:, :, 1, :], res1[:]))
                step(n + 12, nc.vector.tensor_tensor(res2[:], res1[:], cs[:, :, 1, :], ALU.subtract))
                nc.vector.tensor_copy(cs[:, :, 2, :], res2[:]).then_inc(cs_ready, 1)

            def result(c):
                dve.wait_ge(out_tm, c + 1)
                if c >= 2:
                    dve.wait_ge(stored[c % 2], 16 * (c // 2))
                nc.vector.tensor_tensor(ot[c % 2][:], tiles(ps_q), x0[:, c], ALU.add).then_inc(ot_ready, 1)

            scaled(0)
            slot(NI, 0, LAYERS)
            residual(0)
            scaled(1)

            def between():
                residual(1)
                second_norm(0)
            slot(NI + 1, 1, LAYERS, between)
            dve.wait_ge(ld["moe"], MOE_LOADS)
            nc.vector.tensor_copy(sel[:], sel32[:]).then_inc(moe_consts, 1)
            nc.vector.tensor_copy(identb[:], ident[:]).then_inc(moe_consts, 1)
            route_scores(0)
            scaled(2)
            second_norm(1)
            route_ranks(0)
            route_weights(0)
            for i in range(CH * U):
                c, u = divmod(i, U)
                if i == 0:
                    residual(2)
                if i == 1:
                    dve.wait_ge(to_tm["D"], NI)
                    stats("D", NI - 1, tiles(ps_d), EPS_LN)
                if i == 2:
                    normalize("D", NI - 1, tiles(ps_d))
                    second_norm(2)
                if i == 3:
                    route_scores(1)
                if i == 4:
                    route_ranks(1)
                    scaled(3)
                if i == 5:
                    route_weights(1)
                if i == 6:
                    residual(3)
                if i == 7:
                    second_norm(3)
                if i == 8:
                    route_scores(2)
                if i == 9:
                    route_ranks(2)
                if i == 10:
                    route_weights(2)
                if i == 11:
                    route_scores(3)
                if i == 12:
                    route_ranks(3)
                if i == 13:
                    route_weights(3)
                dve.wait_ge(sg_ready, i + 1)
                dve.wait_ge(up_mm, i + 1)
                if i >= 2:
                    dve.wait_ge(down_mm, i - 1)
                if u >= SHARED:
                    nc.vector.tensor_tensor(su[i % 2][:], up_bank[i % 2][:], sg[i % 2][:], ALU.mult).then_inc(su_ready, 1)
                    dve.wait_ge(su_ready, i + 1)
                    dve.wait_ge(bc_mm, routed(i) + 1)
                    nc.vector.tensor_tensor(sc[i % 2][:], ps_d[:], su[i % 2][:], ALU.mult).then_inc(sc_ready, 1)
                else:
                    nc.vector.tensor_tensor(sc[i % 2][:], up_bank[i % 2][:], sg[i % 2][:], ALU.mult).then_inc(su_ready, 1)
                if u == 4 and c:
                    result(c - 1)
                if u == U - 1:
                    dve.wait_ge(down_mm, i + 1)
                    for h in range(HB):
                        b = c * HB + h
                        nc.vector.tensor_scalar(half(yf, h), half(ps_y, h), gt[:, 1, b:b + 1], None,
                                                ALU.mult).then_inc(yf_ready, 1)
            result(CH - 1)


def kernel(**inputs):
    import numpy as np
    import concourse.bacc as bacc
    from concourse.bass_utils import run_bass_kernel_spmd

    def w(name):
        return np.asarray(inputs[name])

    def stack(*names):
        return np.ascontiguousarray(np.stack([w(n) for n in names], axis=-1))

    select = np.zeros((3, E, E, P), np.float32)
    for e in range(E):
        select[:, e, e, :] = 1.0
    lower = np.broadcast_to(np.tril(np.ones((E, E), np.float32), -1).reshape(1, E * E), (P, E * E))
    sg = w("L0_ffn_shared_gate_w").reshape(D, 2, P)
    su = w("L0_ffn_shared_up_w").reshape(D, 2, P)
    sd = w("L0_ffn_shared_down_w").reshape(2, P, D).transpose(1, 0, 2)
    gates = np.concatenate([sg, w("L0_ffn_gate_w").transpose(1, 0, 2)], axis=1)
    ups = np.concatenate([su, w("L0_ffn_up_w").transpose(1, 0, 2)], axis=1)
    downs = np.concatenate([sd, w("L0_ffn_down_w").transpose(1, 0, 2)], axis=1)
    arrays = {
        "x": w("L0_attn_x").reshape(NB * L, D),
        "w_qkv": np.concatenate([w("L0_attn_Wk"), w("L0_attn_Wq"), w("L0_attn_Wv")], axis=2),
        "w_o": w("L0_attn_Wo"),
        "w_f1": w("L0_attn_Wf1"),
        "w_f2": w("L0_attn_Wf2").reshape(LAYERS, FJ, P, D).transpose(0, 2, 1, 3),
        "v_a": stack("L0_attn_bk", "L0_attn_bq", "L0_attn_bv"),
        "v_bo": stack("L0_attn_bo"),
        "v_ln1": stack("L0_attn_ln1_s", "L0_attn_ln1_b"),
        "v_bf1": w("L0_attn_bf1").reshape(LAYERS, FJ, P).transpose(0, 2, 1),
        "v_bf2": stack("L0_attn_bf2"),
        "v_ln2": stack("L0_attn_ln2_s", "L0_attn_ln2_b"),
        "c_t": w("L0_c").T,
        "w_mod": w("L0_wmod"),
        "w_router": w("L0_ffn_router_w"),
        "w_unit": np.stack([gates, ups, downs], axis=2),
        "ident": np.eye(P, dtype=np.float32),
        "select": select.reshape(3 * E, E * P),
        "lower": lower,
    }
    nc = bacc.Bacc("TRN2", target_bir_lowering=False, num_devices=1)
    arrays = {f"in_{k}": np.ascontiguousarray(a) for k, a in arrays.items()}
    args = [nc.dram_tensor(k, a.shape, mybir.dt.from_np(a.dtype), kind="ExternalInput").ap() for k, a in arrays.items()]
    result = nc.dram_tensor("out_0", (NB * L, D), F32, kind="ExternalOutput").ap()
    adaln_block(nc, *args, result)
    r = run_bass_kernel_spmd(nc, [arrays], core_ids=[0])
    return r.results[0]["out_0"].reshape(NB, L, D)
```

```python
import math
from contextlib import ExitStack

import concourse.bass as bass
from concourse import mybir

ALU = mybir.AluOpType
ACT = mybir.ActivationFunctionType
F32 = mybir.dt.float32
F32R = mybir.dt.float32r
BF16 = mybir.dt.bfloat16
AX_X = mybir.AxisListType.X

P = 128
NB, L, D = 8, 256, 128
LAYERS, F = 8, 512
E = 8
G = 512
CH = NB * L // G
HB = G // L
T = G // P
FJ = F // P
NI = LAYERS * CH
SHARED = 2
U = SHARED + E
EPS_LN, EPS_Z, EPS_MOD = 1e-6, 1e-6, 1e-5
LN_SET = "natural_log_exp_and_others"


def adaln_block(nc, x, w_qkv, w_o, w_f1, w_f2, v_a, v_bo, v_ln1, v_bf1, v_bf2, v_ln2, c_t, w_mod,
                w_router, w_unit, ident_in, select_in, lower_in, out):
    with ExitStack() as ctx:
        def sb(name, shape, dt=F32):
            return ctx.enter_context(nc.sbuf_tensor(name, shape, dt))

        def sem(name):
            return ctx.enter_context(nc.semaphore(name))

        ident = sb("ident", [P, P])
        wqkv = sb("wqkv", [P, 3 * P])
        wo = sb("wo", [P, P])
        wf1 = sb("wf1", [P, F])
        wf2 = sb("wf2", [P, FJ, P])
        va = sb("va", [P, 3])
        vbo = sb("vbo", [P, 1])
        vln1 = sb("vln1", [P, 2])
        vbf1 = sb("vbf1", [P, FJ])
        vbf2 = sb("vbf2", [P, 1])
        vln2 = sb("vln2", [P, 2])
        x0 = sb("x0", [P, CH, T, D])
        xs = [sb(f"xs{c}", [P, G]) for c in range(CH)]
        x2 = [sb(f"x2_{c}", [P, G]) for c in range(CH)]
        vt = [sb(f"vt{c}", [P, G]) for c in range(CH)]
        ek, eq = sb("ek", [P, G]), sb("eq", [P, G])
        mk, mq = sb("mk", [P, G]), sb("mq", [P, G])
        kk, qq, kv_full = sb("kk", [P, G]), sb("qq", [P, G]), sb("kv_full", [P, G])
        lden, dd = sb("lden", [P, G]), sb("dd", [P, G])
        elu_k_sb, elu_q_sb, kpos = sb("elu_k_sb", [P, G]), sb("elu_q_sb", [P, G]), sb("kpos", [P, HB])
        ksum, kvsum, rk = sb("ksum", [P, HB]), sb("kvsum", [P, HB]), sb("rk", [P, HB])
        ck, nck = sb("ck", [P, HB]), sb("nck", [P, HB])
        g1, y1, g2, y2 = sb("g1", [P, G]), sb("y1", [P, G]), sb("g2", [P, G]), sb("y2", [P, G])
        hid = sb("hid", [P, FJ, G])
        xh = {k: sb(f"xh{k}", [P, T, D]) for k in "BDF"}
        rows = ["I0", "I1", "I2", "I3", "B", "D", "F0", "F1"]
        st = {k: sb(f"st{k}", [P, T, 6]) for k in rows}
        dif, sq, dif2, mean = ({k: sb(f"{name}{k}", [P, T]) for k in rows}
                                   for name in ("dif", "sq", "dif2", "mean"))
        ve = {k: sb(f"ve{k}", [P, T]) for k in rows}
        rs = {k: sb(f"rs{k}", [P, T]) for k in rows}
        ones = sb("ones", [P, G])
        c_eps, c_lneps, c_half = sb("c_eps", [P, 1]), sb("c_lneps", [P, 1]), sb("c_half", [P, T])
        ct, sct = sb("ct", [P, NB]), sb("sct", [P, NB])
        wmod = sb("wmod", [P, 6 * D])
        mod = sb("mod", [P, 6, NB])
        m1 = sb("m1", [P, 2, NB])
        gt = sb("gt", [P, 2, NB])
        gsg, gab = sb("gsg", [P, 2, NB]), sb("gab", [P, 2, NB])
        wr = sb("wr", [P, E])
        wu = sb("wu", [P, U, 3, P])
        wu_hi, wu_lo = sb("wu_hi", [P, U, 3, P], F32R), sb("wu_lo", [P, U, 3, P], F32R)
        h_hi = [sb(f"h_hi{i}", [P, G], F32R) for i in range(2)]
        h_lo = [sb(f"h_lo{i}", [P, G], F32R) for i in range(2)]
        sel32, sel = sb("sel32", [3 * E, E * P]), sb("sel", [3 * E, E * P], BF16)
        lower = sb("lower", [P, E * E])
        zf = sb("zf", [P, G])
        hf = [sb(f"hf{c}", [P, G]) for c in range(CH)]
        mx, lg, ex = sb("mx", [P, T]), sb("lg", [P, T, E]), sb("ex", [P, T, E])
        sm, rsm = sb("sm", [P, T]), sb("rsm", [P, T])
        cmp_gt, cmp_eq = sb("cmp_gt", [P, T, E * E]), sb("cmp_eq", [P, T, E * E])
        cmp_lo, cmp_all = sb("cmp_lo", [P, T, E * E]), sb("cmp_all", [P, T, E * E])
        rank, comb, comb2 = sb("rank", [P, T, E]), sb("comb", [P, T, E]), sb("comb2", [P, T, E])
        res1, res2 = sb("res1", [P, T, E]), sb("res2", [P, T, E])
        cs = sb("cs", [P, T, 3, E], BF16)
        identb = sb("identb", [P, P], BF16)
        cst = [sb(f"cst{c}", [3 * E, G], BF16) for c in range(CH)]
        sg = [sb(f"sg{i}", [P, G]) for i in range(2)]
        su = [sb(f"su{i}", [P, G]) for i in range(2)]
        sc = [sb(f"sc{i}", [P, G]) for i in range(3)]
        sc_hi = [sb(f"sc_hi{i}", [P, G], F32R) for i in range(2)]
        sc_lo = [sb(f"sc_lo{i}", [P, G], F32R) for i in range(2)]
        yf = sb("yf", [P, G])
        ot = [sb(f"ot{i}", [P, T, D]) for i in range(2)]

        bank = [ctx.enter_context(nc.psum_tensor(f"bank{i}", [P, G], F32)) for i in range(8)]
        ps_k, ps_q, ps_v, ps_f0, ps_f1, ps_b, ps_d, ps_y = bank
        ps_ff = [ps_f0, ps_f1, ps_y, ps_k]

        gate_bank, up_bank = [ps_k, ps_f1], [ps_b, ps_f0]

        def gates(i):
            return gate_bank[i % 2] if i else ps_v

        ld = {k: sem(f"ld_{k}") for k in ("const", "mod", "moe", "wqkv", "va", "wo", "vbo", "vln1",
                                          "wf1", "vbf1", "wf2", "vbf2", "vln2")}
        ld["x0"] = [sem(f"ld_x0_{c}") for c in range(CH)]
        consts_set = sem("consts_set")
        silu_c, mod_mm, mod_copied, mod_done = sem("silu_c"), sem("mod_mm"), sem("mod_copied"), sem("mod_done")
        ga_parts = sem("ga_parts")
        k_mm, q_mm, v_mm = sem("k_mm"), sem("q_mm"), sem("v_mm")
        ek_ready, eq_ready = sem("ek_ready"), sem("eq_ready")
        elu_k, elu_q, kpos_ready = sem("elu_k"), sem("elu_q"), sem("kpos_ready")
        mk_ready, k_ready, mq_ready, q_ready = sem("mk_ready"), sem("k_ready"), sem("mq_ready"), sem("q_ready")
        rk_ready, kv_ready, ck_ready, nck_ready = sem("rk_ready"), sem("kv_ready"), sem("ck_ready"), sem("nck_ready")
        lden_ready, dd_ready, v_ready = sem("lden_ready"), sem("dd_ready"), sem("v_ready")
        wo_mm, g1_ready, y1_ready = sem("wo_mm"), sem("g1_ready"), sem("y1_ready")
        ff1_mm, h_ready, ff2_mm, g2_ready, y2_ready = (sem("ff1_mm"), sem("h_ready"), sem("ff2_mm"),
                                                       sem("g2_ready"), sem("y2_ready"))
        x2_ready, x_ready = sem("x2_ready"), sem("x_ready")
        to_tm = {k: sem(f"to_tm{k}") for k in "BDF"}
        bn_done = {k: sem(f"bn_done{k}") for k in "IBDF"}
        agg_done = {k: sem(f"agg_done{k}") for k in "IBDF"}
        var_ready = {k: sem(f"var_ready{k}") for k in "IBDF"}
        rstd_ready = {k: sem(f"rstd_ready{k}") for k in "IBDF"}
        normed = {k: sem(f"normed{k}") for k in "IBDF"}
        to_fm = {k: sem(f"to_fm{k}") for k in "IBDF"}
        zf_ready, x_new, hf_ready = sem("zf_ready"), sem("x_new"), sem("hf_ready")
        moe_consts, score_mm = sem("moe_consts"), sem("score_mm")
        lg_ready, ex_ready = sem("lg_ready"), sem("ex_ready")
        rt = sem("rt")
        cs_ready, cst_mm, cst_ready = sem("cs_ready"), sem("cst_mm"), sem("cst_ready")
        gate_mm, up_mm, bc_mm, down_mm = sem("gate_mm"), sem("up_mm"), sem("bc_mm"), sem("down_mm")
        wu_hi_ready, wu_lo_ready = sem("wu_hi_ready"), sem("wu_lo_ready")
        h_hi_ready, h_lo_ready = sem("h_hi_ready"), sem("h_lo_ready")
        sg_ready, su_ready, sc_ready = sem("sg_ready"), sem("su_ready"), sem("sc_ready")
        sc_hi_ready, sc_lo_ready = sem("sc_hi_ready"), sem("sc_lo_ready")
        yf_ready, out_tm, ot_ready = sem("yf_ready"), sem("out_tm"), sem("ot_ready")
        stored = [sem(f"stored{i}") for i in range(2)]

        x_rows = x.rearrange("(c h p j) d -> p c h j d", c=CH, h=HB, p=P)
        out_rows = out.rearrange("(c h p j) d -> p c h j d", c=CH, h=HB, p=P)

        def buf(k, n):
            return f"F{n % 2}" if k == "F" else f"I{n}" if k == "I" else k

        def rows_of(k, n):
            return hf[n][:].rearrange("p (t d) -> p t d", t=T) if k == "I" else xh[k][:]

        def half(ap, h):
            return ap[:, h * L:(h + 1) * L]

        def has(n):
            return not isinstance(n, int) or 0 <= n < NI

        def wait(eng, s, value):
            if not isinstance(value, int) or value > 0:
                eng.wait_ge(s, value)

        def routed(i):
            return i // U * E + max(i % U - SHARED, 0)

        def run(extra, place):
            if extra and place in extra:
                extra[place]()

        def splits(i):
            return min(max(i - U, 0), CH * U - U - 2)

        def unit_done(eng, i):
            if i % U >= SHARED:
                eng.wait_ge(sc_ready, routed(i) + 1)
            else:
                eng.wait_ge(su_ready, i + 1)

        def slots(eng, one_slot, extra=None):
            one_slot(0, 0, 0, extra)
            for s in range(1, CH - 1):
                one_slot(s, s % CH, s // CH)
            with eng.Fori(0, LAYERS - 1) as i:
                for j in range(CH):
                    s = CH - 1 + j
                    one_slot(i * CH + s, s % CH, i + s // CH)
            one_slot(NI - 1, CH - 1, LAYERS - 1)

        block = ctx.enter_context(nc.Block())

        @block.sync
        def _(sp):
            for c in range(CH):
                x0_rows = x0[:, c, :, :].rearrange("p (h j) d -> p h j d", h=HB)
                sp.dma_start(x0_rows, x_rows[:, c]).then_inc(ld["x0"][c], 16)
                if c == 0:
                    sp.dma_start(ident[:], ident_in).then_inc(ld["const"], 16)

            def layer_loads(l, first):
                if not first:
                    sp.wait_ge(v_mm, CH * l)
                    sp.dma_start(wqkv[:], w_qkv[l]).then_inc(ld["wqkv"], 16)
                    sp.wait_ge(kv_ready, CH * l)
                    sp.wait_ge(elu_q, CH * l)
                    sp.dma_start(va[:], v_a[l]).then_inc(ld["va"], 16)
                if not first:
                    sp.wait_ge(wo_mm, CH * l)
                sp.dma_start(wo[:], w_o[l]).then_inc(ld["wo"], 16)
                if not first:
                    sp.wait_ge(g1_ready, CH * l)
                sp.dma_start(vbo[:], v_bo[l]).then_inc(ld["vbo"], 16)
                if not first:
                    sp.wait_ge(x2_ready, HB * CH * l)
                sp.dma_start(vln1[:], v_ln1[l]).then_inc(ld["vln1"], 16)
                if not first:
                    sp.wait_ge(ff1_mm, FJ * CH * l)
                sp.dma_start(wf1[:], w_f1[l]).then_inc(ld["wf1"], 16)
                if not first:
                    sp.wait_ge(h_ready, FJ * CH * l)
                sp.dma_start(vbf1[:], v_bf1[l]).then_inc(ld["vbf1"], 16)
                if not first:
                    sp.wait_ge(ff2_mm, CH * l)
                sp.dma_start(wf2[:], w_f2[l]).then_inc(ld["wf2"], 16)
                if not first:
                    sp.wait_ge(g2_ready, CH * l)
                sp.dma_start(vbf2[:], v_bf2[l]).then_inc(ld["vbf2"], 16)
                if not first:
                    sp.wait_ge(x_ready, CH * l + CH)
                sp.dma_start(vln2[:], v_ln2[l]).then_inc(ld["vln2"], 16)

            layer_loads(0, True)
            sp.dma_start(wr[:], w_router).then_inc(ld["moe"], 16)
            sp.dma_start(sel32[:], select_in).then_inc(ld["moe"], 16)
            sp.dma_start(lower[:], lower_in).then_inc(ld["moe"], 16)
            for u in range(U):
                sp.dma_start(wu[:, u], w_unit[:, u]).then_inc(ld["moe"], 16)
            with sp.Fori(1, LAYERS) as l:
                layer_loads(l, False)
            for c in range(CH):
                sp.wait_ge(ot_ready, c + 1)
                ot_rows = ot[c % 2][:, :, :].rearrange("p (h j) d -> p h j d", h=HB)
                sp.dma_start(out_rows[:, c], ot_rows).then_inc(stored[c % 2], 16)
            for i in range(2):
                sp.wait_ge(stored[i], 16 * CH // 2)

        MOE_LOADS = 16 * (3 + U)

        @block.tensor
        def _(pe):
            def transposes(out_bank, src, done):
                for j in range(T):
                    t = src[:, j, :] if len(src.shape) == 3 else src[:, j * P:(j + 1) * P]
                    mm = nc.tensor.transpose(out_bank[:, j * P:(j + 1) * P], t, ident[:])
                mm.then_inc(done, 1)

            pe.wait_ge(ld["const"], 16)
            pe.wait_ge(ld["mod"], 32)
            pe.wait_ge(silu_c, 1)
            for m in range(6):
                mm = nc.tensor.matmul(ps_y[:, m * NB:(m + 1) * NB], wmod[:, m * D:(m + 1) * D], sct[:],
                                      start=True, stop=True)
            mm.then_inc(mod_mm, 1)

            def first_to_fm(c):
                pe.wait_ge(normed["I"], c + 1)
                transposes([ps_f0, ps_f1, ps_b, ps_d][c], rows_of("I", c), to_fm["I"])

            def rest_to_fm():
                for c in range(1, CH):
                    first_to_fm(c)

            first_to_fm(0)

            def slot(s, c, l, extra=None):
                a, b, f, d = s, s - 1, s - 2, s - 3
                if has(a):
                    pe.wait_ge(x_ready, a + 1)
                    if c == 0:
                        pe.wait_ge(ld["wqkv"], 4 * a + 16)
                    if has(a - 3):
                        pe.wait_ge(h_ready, 4 * (a - 3) + 4)
                    elif has(a - 1):
                        pe.wait_ge(elu_k, a)
                    nc.tensor.matmul(ps_k[:], wqkv[:, 0:P], xs[c][:], start=True, stop=True).then_inc(k_mm, 1)
                    if has(a - 1):
                        pe.wait_ge(elu_q, a)
                    nc.tensor.matmul(ps_q[:], wqkv[:, P:2 * P], xs[c][:], start=True, stop=True).then_inc(q_mm, 1)
                    if has(a - 1):
                        pe.wait_ge(kv_ready, a)
                    nc.tensor.matmul(half(ps_v, 0), wqkv[:, 2 * P:3 * P], half(xs[c], 0), start=True, stop=True)
                if has(f):
                    pe.wait_ge(normed["B"], f + 1)
                    transposes(ps_b, xh["B"], to_fm["B"])
                if has(a):
                    nc.tensor.matmul(half(ps_v, 1), wqkv[:, 2 * P:3 * P], half(xs[c], 1),
                                     start=True, stop=True).then_inc(v_mm, 1)
                run(extra, "start")

                def last_norm_to_tm():
                    pe.wait_ge(y2_ready, d + 1)
                    pe.wait_ge(x_ready, d + CH)
                    transposes(ps_d, y2, to_tm["D"])

                if has(d) and has(b):
                    last_norm_to_tm()

                def ff1(j):
                    if j == 0:
                        wait(pe, g2_ready, f)
                        if isinstance(f, int) and f == 0:
                            pe.wait_ge(mod_copied, 1)
                        if (c - 2) % CH == 0:
                            pe.wait_ge(ld["wf1"], 4 * f + 16)
                    if j == 3:
                        pe.wait_ge(elu_k, a + 1 if has(a) else NI)
                        if not has(a):
                            pe.wait_ge(h_ready, 4 * f)
                    if j == 0:
                        for h in range(HB):
                            pe.wait_ge(x2_ready, HB * f + h + 1)
                            mm = nc.tensor.matmul(half(ps_ff[0], h), wf1[:, 0:P], half(x2[(c - 2) % CH], h),
                                                  start=True, stop=True)
                    else:
                        mm = nc.tensor.matmul(ps_ff[j][:], wf1[:, j * P:(j + 1) * P], x2[(c - 2) % CH][:],
                                              start=True, stop=True)
                    mm.then_inc(ff1_mm, 1)

                def ff2(j):
                    if j == 0 and (c - 2) % CH == 0:
                        pe.wait_ge(ld["wf2"], 4 * f + 16)
                    pe.wait_ge(h_ready, 4 * f + j + 1)
                    mm = nc.tensor.matmul(ps_f0[:], wf2[:, j, :], hid[:, j, :], start=(j == 0), stop=(j == FJ - 1))
                    if j == FJ - 1:
                        mm.then_inc(ff2_mm, 1)

                if has(f):
                    ff1(0)
                    ff1(1)
                    ff1(2)
                if has(b):
                    pe.wait_ge(v_ready, b + 1)
                    if (c - 1) % CH == 0:
                        pe.wait_ge(ld["wo"], 4 * b + 16)
                    wait(pe, x2_ready, HB * b)
                    if isinstance(b, int) and b == 0:
                        pe.wait_ge(x_ready, CH)
                    nc.tensor.matmul(ps_b[:], wo[:], vt[(c - 1) % CH][:], start=True, stop=True).then_inc(wo_mm, 1)
                if has(d) and not has(b):
                    last_norm_to_tm()
                run(extra, "before ff2")
                if has(f):
                    ff2(0)
                    ff1(3)
                run(extra, "middle")
                if has(f):
                    ff2(1)
                if has(b):
                    pe.wait_ge(y1_ready, b + 1)
                    transposes(ps_b, y1, to_tm["B"])
                if has(d):
                    pe.wait_ge(normed["D"], d + 1)
                    transposes(ps_d, xh["D"], to_fm["D"])
                if has(f):
                    ff2(2)
                    ff2(3)

            slots(pe, slot, {"middle": rest_to_fm})

            last = NI - 1

            def zf_to_tm(c):
                pe.wait_ge(zf_ready, c + 1)
                if c == 0:
                    pe.wait_ge(elu_q, NI)
                if c:
                    pe.wait_ge(lg_ready, c)
                if c > 2:
                    pe.wait_ge(ot_ready, c - 2)
                transposes(ps_q, zf, to_tm["F"])

            def norm_to_fm(c):
                pe.wait_ge(normed["F"], c + 1)
                if c == 0:
                    pe.wait_ge(kv_ready, NI)
                if c:
                    pe.wait_ge(cst_ready, c)
                if c == 2:
                    pe.wait_ge(x_ready, NI + CH)
                transposes(ps_v, xh["F"], to_fm["F"])

            def scores(c):
                pe.wait_ge(hf_ready, c + 1)
                pe.wait_ge(x_new, c + 1)
                if c > 1:
                    pe.wait_ge(ot_ready, c - 1)
                for j in range(T):
                    mm = nc.tensor.matmul(ps_q[:, j * E:(j + 1) * E], hf[c][:, j * P:(j + 1) * P], wr[:],
                                          start=True, stop=True)
                mm.then_inc(score_mm, 1)

            def weights_to_fm(c):
                pe.wait_ge(moe_consts, 2)
                pe.wait_ge(cs_ready, c + 1)
                pe.wait_ge(hf_ready, c + 1)
                if c == 0:
                    pe.wait_ge(sg_ready, 1)
                psb = ps_v[:].bitcast(BF16)
                for j in range(T):
                    mm = nc.tensor.transpose(psb[0:3 * E, j * P:(j + 1) * P],
                                             cs[:, j, :, :].rearrange("p a e -> p (a e)"), identb[:])
                mm.then_inc(cst_mm, 1)

            def last_to_tm():
                pe.wait_ge(y2_ready, NI)
                pe.wait_ge(hf_ready, 2)
                pe.wait_ge(cst_ready, 2)
                transposes(ps_v, y2, to_tm["D"])

            def last_to_fm():
                pe.wait_ge(normed["D"], NI)
                transposes(ps_v, xh["D"], to_fm["D"])

            def product(bank, i, m):
                c, u = divmod(i, U)
                if c == 0:
                    return nc.tensor.matmul(bank[:], wu[:, u, m, :], hf[0][:], start=True, stop=True)
                nc.tensor.matmul(bank[:], wu_hi[:, u, m, :], h_hi[c % 2][:], start=True, stop=False)
                nc.tensor.matmul(bank[:], wu_lo[:, u, m, :], h_hi[c % 2][:], start=False, stop=False)
                return nc.tensor.matmul(bank[:], wu_hi[:, u, m, :], h_lo[c % 2][:], start=False, stop=True)

            def gate(i):
                c, u = divmod(i, U)
                if i == 0:
                    pe.wait_ge(hf_ready, 1)
                if c == 1:
                    pe.wait_ge(wu_hi_ready, u + 1)
                    pe.wait_ge(wu_lo_ready, u + 1)
                if c and u == 0:
                    pe.wait_ge(h_hi_ready, c)
                    pe.wait_ge(h_lo_ready, c)
                if i in (1, 2):
                    pe.wait_ge(h_ready, FJ * NI)
                if i >= 2:
                    pe.wait_ge(sg_ready, i - 1)
                product(gates(i), i, 0).then_inc(gate_mm, 1)

            def up(i):
                c, u = divmod(i, U)
                if i == 0:
                    pe.wait_ge(x2_ready, HB * NI)
                if i == 1:
                    pe.wait_ge(g2_ready, NI)
                if i >= 2:
                    pe.wait_ge(su_ready, i - 1)
                product(up_bank[i % 2], i, 1).then_inc(up_mm, 1)

            def down(i):
                c, u = divmod(i, U)
                if u == 0 and c:
                    pe.wait_ge(yf_ready, HB * c)
                if i == 0:
                    pe.wait_ge(h_ready, FJ * NI)
                if splits(i + 1) == splits(i):
                    unit_done(pe, i)
                    mm = nc.tensor.matmul(ps_y[:], wu[:, u, 2, :], sc[i % 3][:], start=(u == 0), stop=(u == U - 1))
                else:
                    k = splits(i)
                    pe.wait_ge(sc_hi_ready, k + 1)
                    nc.tensor.matmul(ps_y[:], wu_hi[:, u, 2, :], sc_hi[k % 2][:], start=(u == 0), stop=False)
                    nc.tensor.matmul(ps_y[:], wu_lo[:, u, 2, :], sc_hi[k % 2][:], start=False, stop=False)
                    pe.wait_ge(sc_lo_ready, k + 1)
                    mm = nc.tensor.matmul(ps_y[:], wu_hi[:, u, 2, :], sc_lo[k % 2][:], start=False, stop=(u == U - 1))
                mm.then_inc(down_mm, 1)

            def broadcast(i):
                c, u = divmod(i, U)
                if u == SHARED:
                    pe.wait_ge(cst_ready, c + 1)
                if i == SHARED:
                    pe.wait_ge(x_ready, NI + CH - 1)
                if routed(i):
                    pe.wait_ge(sc_ready, routed(i))
                e = u - SHARED
                nc.tensor.matmul(ps_d[:], sel[:, e * P:(e + 1) * P], cst[c][:],
                                 start=True, stop=True).then_inc(bc_mm, 1)

            def result_to_tm(c):
                pe.wait_ge(yf_ready, HB * (c + 1))
                pe.wait_ge(lg_ready, min(c + 2, CH))
                pe.wait_ge(x_new, min(c + 3, CH))
                if c:
                    pe.wait_ge(ot_ready, c)
                transposes(ps_q, yf, out_tm)

            def scores_0():
                pe.wait_ge(ld["moe"], MOE_LOADS)
                scores(0)

            def unit_0():
                gate(0)
                up(0)

            slot(NI, 0, LAYERS, {"start": lambda: zf_to_tm(0)})
            norm_to_fm(0)
            slot(NI + 1, 1, LAYERS, {"start": scores_0, "before ff2": unit_0})
            for i in range(CH * U):
                c, u = divmod(i, U)
                n = c + 1
                if u == 3 and n < CH:
                    zf_to_tm(n)
                if i == U + 2:
                    last_to_tm()
                if i:
                    gate(i)
                    up(i)
                    if u == 1:
                        weights_to_fm(c)
                    if i == U + 4:
                        last_to_fm()
                    if u == 6 and n < CH:
                        norm_to_fm(n)
                    if u == 7 and n < CH:
                        scores(n)
                    if i > 1:
                        down(i - 2)
                if u >= SHARED:
                    broadcast(i)
                if u == 4 and c:
                    result_to_tm(c - 1)
            down(CH * U - 2)
            down(CH * U - 1)
            result_to_tm(CH - 1)

        @block.scalar
        def _(act):
            act.dma_start(ct[:], c_t).then_inc(ld["mod"], 16)
            act.dma_start(wmod[:], w_mod).then_inc(ld["mod"], 16)
            act.dma_start(wqkv[:], w_qkv[0]).then_inc(ld["wqkv"], 16)
            act.dma_start(va[:], v_a[0]).then_inc(ld["va"], 16)
            act.wait_ge(ld["mod"], 32)
            nc.scalar.activation(sct[:], ct[:], ACT.Silu).then_inc(silu_c, 1)
            act.wait_ge(mod_done, 1)
            def first_norm(c):
                act.wait_ge(to_fm["I"], c + 1)
                for h in range(HB):
                    b = c * HB + h
                    ev = nc.scalar.activation(half(xs[c], h), half([ps_f0, ps_f1, ps_b, ps_d][c], h), ACT.Identity,
                                              bias=mod[:, 0, b:b + 1], scale=m1[:, 0, b:b + 1])
                ev.then_inc(x_ready, 1)

            def rest_of_first_norm():
                for c in range(1, CH):
                    first_norm(c)

            first_norm(0)
            act.wait_ge(consts_set, 4)

            def slot(s, c, l, extra=None):
                a, b, f, d = s, s - 1, s - 2, s - 3
                if has(d):
                    act.wait_ge(ff2_mm, d + 1)
                    if (c - 3) % CH == 0:
                        act.wait_ge(ld["vbf2"], 4 * d + 16)
                    nc.scalar.activation(g2[:], ps_f0[:], ACT.Gelu_apprx_tanh, bias=vbf2[:, 0:1]).then_inc(g2_ready, 1)
                run(extra, "start")
                if (has(a) or has(b)) and not (isinstance(s, int) and s == 1):
                    nc.scalar.preload_act_table_set(LN_SET)
                if has(b):
                    act.wait_ge(q_ready, b + 1)
                    act.wait_ge(k_ready, b + 1)
                    for h in range(HB):
                        ln = nc.scalar.activation(half(lden, h), half(qq, h), ACT.Ln,
                                                  bias=c_eps[:, 0:1], scale=ksum[:, h:h + 1])
                    ln.then_inc(lden_ready, 1)
                    act.wait_ge(lden_ready, b + 1)
                    nc.scalar.activation(dd[:], lden[:], ACT.Exp, bias=c_lneps[:, 0:1], scale=-1.0).then_inc(dd_ready, 1)
                if has(a):
                    act.wait_ge(k_mm, a + 1)
                    if c == 0:
                        act.wait_ge(ld["va"], 4 * a + 16)
                    nc.scalar.activation(ek[:], ps_k[:], ACT.Exp, bias=va[:, 0:1]).then_inc(ek_ready, 1)
                    act.wait_ge(q_mm, a + 1)
                    nc.scalar.activation(eq[:], ps_q[:], ACT.Exp, bias=va[:, 1:2]).then_inc(eq_ready, 1)
                for j in range(FJ):
                    if has(f):
                        act.wait_ge(ff1_mm, 4 * f + j + 1)
                        if j == 0 and (c - 2) % CH == 0:
                            act.wait_ge(ld["vbf1"], 4 * f + 16)
                        nc.scalar.activation(hid[:, j, :], ps_ff[j][:], ACT.Gelu_apprx_tanh,
                                             bias=vbf1[:, j:j + 1]).then_inc(h_ready, 1)
                    if j == 0 and has(b):
                        act.wait_ge(wo_mm, b + 1)
                        if (c - 1) % CH == 0:
                            act.wait_ge(ld["vbo"], 4 * b + 16)
                        nc.scalar.activation(g1[:], ps_b[:], ACT.Gelu_apprx_tanh, bias=vbo[:, 0:1]).then_inc(g1_ready, 1)
                    if j == 1:
                        run(extra, "middle")
                    if j == 3 and has(d):
                        act.wait_ge(to_fm["D"], d + 1)
                        if (c - 3) % CH == 0:
                            act.wait_ge(ld["vln2"], 4 * d + 16)
                        nc.scalar.activation(xs[(c - 3) % CH][:], ps_d[:], ACT.Identity,
                                             bias=vln2[:, 1:2], scale=vln2[:, 0:1]).then_inc(x_ready, 1)

            slots(act, slot, {"middle": rest_of_first_norm})
            def second_norm(c):
                act.wait_ge(to_fm["F"], c + 1)
                for h in range(HB):
                    b = c * HB + h
                    ev = nc.scalar.activation(half(hf[c], h), half(ps_v, h), ACT.Identity,
                                              bias=mod[:, 3, b:b + 1], scale=m1[:, 1, b:b + 1])
                ev.then_inc(hf_ready, 1)

            def exponentials(c):
                act.wait_ge(lg_ready, c + 1)
                nc.scalar.activation(ex[:], lg[:], ACT.Exp).then_inc(ex_ready, 1)

            def weights(c):
                act.wait_ge(cst_mm, c + 1)
                nc.scalar.activation(cst[c][:], ps_v[:].bitcast(BF16)[0:3 * E, 0:G], ACT.Copy).then_inc(cst_ready, 1)

            def first_scores():
                second_norm(0)
                exponentials(0)

            slot(NI, 0, LAYERS)
            slot(NI + 1, 1, LAYERS, {"start": first_scores})
            act.wait_ge(ff2_mm, NI)
            nc.scalar.activation(g2[:], ps_f0[:], ACT.Gelu_apprx_tanh, bias=vbf2[:, 0:1]).then_inc(g2_ready, 1)
            for i in range(CH * U):
                c, u = divmod(i, U)
                n = c + 1
                act.wait_ge(gate_mm, i + 1)
                if i >= 2:
                    act.wait_ge(su_ready, i - 1)
                nc.scalar.activation(sg[i % 2][:], gates(i)[:], ACT.Silu).then_inc(sg_ready, 1)
                if splits(i) > splits(i - 1):
                    k = splits(i - 1)
                    unit_done(act, i - 1)
                    if k >= 2:
                        act.wait_ge(down_mm, i - 2)
                        act.wait_ge(sc_lo_ready, k - 1)
                    nc.scalar.activation(sc_hi[k % 2][:], sc[(i - 1) % 3][:], ACT.Copy).then_inc(sc_hi_ready, 1)
                if i == U + 4:
                    act.wait_ge(to_fm["D"], NI)
                    nc.scalar.activation(xs[CH - 1][:], ps_v[:], ACT.Identity,
                                         bias=vln2[:, 1:2], scale=vln2[:, 0:1]).then_inc(x_ready, 1)
                if u == 6 and n < CH:
                    second_norm(n)
                    act.wait_ge(hf_ready, n + 1)
                    if n > 2:
                        act.wait_ge(up_mm, (n - 1) * U)
                        act.wait_ge(h_lo_ready, n - 2)
                    nc.scalar.activation(h_hi[n % 2][:], hf[n][:], ACT.Copy).then_inc(h_hi_ready, 1)
                if u == 8 and n < CH:
                    exponentials(n)
                if u == 1:
                    weights(c)
                if c == 0:
                    nc.scalar.activation(wu_hi[:, u, :, :], wu[:, u, :, :], ACT.Copy).then_inc(wu_hi_ready, 1)

        @block.gpsimd
        def _(pool):
            nc.gpsimd.memset(ones[:], 1.0).then_inc(consts_set, 1)
            nc.gpsimd.memset(c_half[:], -0.5).then_inc(consts_set, 1)
            nc.gpsimd.memset(c_eps[:], EPS_Z).then_inc(consts_set, 1)
            nc.gpsimd.memset(c_lneps[:], math.log(EPS_Z)).then_inc(consts_set, 1)
            pool.wait_ge(consts_set, 4)

            def rstd(k, n):
                pool.wait_ge(var_ready[k], n + 1)
                nc.gpsimd.tensor_tensor(rs[buf(k, n)][:], ve[buf(k, n)][:], c_half[:], ALU.pow).then_inc(rstd_ready[k], 1)

            for c in range(CH):
                rstd("I", c)

            def slot(s, c, l, extra=None):
                a, b, d = s, s - 1, s - 3
                if has(d):
                    pool.wait_ge(g2_ready, d + 1)
                    nc.gpsimd.tensor_tensor(y2[:], g2[:], x2[(c - 3) % CH][:], ALU.add).then_inc(y2_ready, 1)
                    rstd("D", d)
                if has(b):
                    pool.wait_ge(g1_ready, b + 1)
                    nc.gpsimd.tensor_tensor(y1[:], g1[:], xs[(c - 1) % CH][:], ALU.add).then_inc(y1_ready, 1)
                if has(a):
                    pool.wait_ge(elu_q, a + 1)
                    nc.gpsimd.tensor_tensor(qq[:], elu_q_sb[:], ones[:], ALU.add).then_inc(q_ready, 1)
                run(extra, "end")
                if has(b):
                    rstd("B", b)

            slots(pool, slot)
            slot(NI, 0, LAYERS, {"end": lambda: rstd("F", 0)})
            slot(NI + 1, 1, LAYERS)
            pool.wait_ge(g2_ready, NI)
            nc.gpsimd.tensor_tensor(y2[:], g2[:], x2[CH - 1][:], ALU.add).then_inc(y2_ready, 1)

            def split_weights(u):
                pool.wait_ge(wu_hi_ready, u + 1)
                nc.gpsimd.tensor_tensor(wu_lo[:, u, :, :], wu[:, u, :, :], wu_hi[:, u, :, :].bitcast(F32),
                                        ALU.subtract).then_inc(wu_lo_ready, 1)

            def split_h(c):
                if c > 2:
                    pool.wait_ge(up_mm, (c - 1) * U)
                pool.wait_ge(h_hi_ready, c)
                nc.gpsimd.tensor_tensor(h_lo[c % 2][:], hf[c][:], h_hi[c % 2][:].bitcast(F32),
                                        ALU.subtract).then_inc(h_lo_ready, 1)

            for u in range(4):
                split_weights(u)
            rstd("F", 1)
            for u in range(4, 7):
                split_weights(u)
            split_h(1)
            for u in range(7, U):
                split_weights(u)
            for i in range(U, CH * U - 2):
                c, u = divmod(i, U)
                n = c + 1
                if i == U + 2:
                    rstd("D", NI - 1)
                if n < CH:
                    if u == 4:
                        rstd("F", n)
                    if u == 7:
                        split_h(n)
                k = splits(i)
                pool.wait_ge(sc_hi_ready, k + 1)
                if k >= 2:
                    pool.wait_ge(down_mm, i - 1)
                nc.gpsimd.tensor_tensor(sc_lo[k % 2][:], sc[i % 3][:], sc_hi[k % 2][:].bitcast(F32),
                                        ALU.subtract).then_inc(sc_lo_ready, 1)

        @block.vector
        def _(dve):
            def stats(k, n, src, eps):
                q = buf(k, n)
                for j in range(T):
                    bn = nc.vector.bn_stats(st[q][:, j, :], src[:, j, :])
                bn.then_inc(bn_done[k], 1)
                dve.wait_ge(bn_done[k], n + 1)
                s_even, s_odd = st[q][:, :, 1:3], st[q][:, :, 4:6]
                nc.vector.tensor_tensor(dif[q][:], s_even[:, :, 0], s_odd[:, :, 0], ALU.subtract)
                nc.vector.scalar_tensor_tensor(out=sq[q][:], in0=s_even[:, :, 1], scalar=D * eps, in1=s_odd[:, :, 1],
                                               op0=ALU.add, op1=ALU.add).then_inc(agg_done[k], 1)
                dve.wait_ge(agg_done[k], 3 * n + 1)
                nc.vector.scalar_tensor_tensor(out=dif2[q][:], in0=dif[q][:], scalar=0.25, in1=dif[q][:],
                                               op0=ALU.mult, op1=ALU.mult).then_inc(agg_done[k], 1)
                dve.wait_ge(agg_done[k], 3 * n + 2)
                nc.vector.scalar_tensor_tensor(out=ve[q][:], in0=sq[q][:], scalar=1.0 / D, in1=dif2[q][:],
                                               op0=ALU.mult, op1=ALU.add).then_inc(var_ready[k], 1)
                nc.vector.scalar_tensor_tensor(out=mean[q][:], in0=dif[q][:], scalar=-0.5, in1=s_even[:, :, 0],
                                               op0=ALU.mult, op1=ALU.add).then_inc(agg_done[k], 1)

            def normalize(k, n, src):
                q = buf(k, n)
                dve.wait_ge(agg_done[k], 3 * n + 3)
                dve.wait_ge(rstd_ready[k], n + 1)
                for j in range(T):
                    ap = nc.vector.tensor_scalar(rows_of(k, n)[:, j, :], src[:, j, :], mean[q][:, j:j + 1], rs[q][:, j:j + 1],
                                                 ALU.subtract, ALU.mult)
                ap.then_inc(normed[k], 1)

            def tiles(ps):
                return ps[:].rearrange("p (t d) -> p t d", t=T)

            def modulation():
                dve.wait_ge(mod_mm, 1)
                nc.vector.tensor_copy(mod[:].rearrange("p m b -> p (m b)"), ps_y[:, 0:6 * NB]).then_inc(mod_copied, 1)
                dve.wait_ge(mod_copied, 1)
                for i, (cc, gg) in enumerate(((1, 2), (4, 5))):
                    nc.vector.tensor_scalar(m1[:, i, :], mod[:, cc, :], 1.0, None, ALU.add).then_inc(ga_parts, 1)
                    nc.vector.tensor_scalar(gsg[:, i, :], mod[:, gg, :], 0.0, 2.0, ALU.is_ge, ALU.mult).then_inc(ga_parts, 1)
                    nc.vector.scalar_tensor_tensor(out=gab[:, i, :], in0=mod[:, gg, :], scalar=-1.0, in1=mod[:, gg, :],
                                                   op0=ALU.mult, op1=ALU.max).then_inc(ga_parts, 1)
                dve.wait_ge(ga_parts, 6)
                nc.vector.tensor_scalar(gab[:], gab[:], 0.25, None, ALU.max).then_inc(ga_parts, 1)
                dve.wait_ge(ga_parts, 7)
                nc.vector.scalar_tensor_tensor(out=gt[:], in0=gsg[:], scalar=-1.0, in1=gab[:],
                                               op0=ALU.add, op1=ALU.mult).then_inc(mod_done, 1)

            for c in range(CH):
                dve.wait_ge(ld["x0"][c], 16)
                stats("I", c, x0[:, c], EPS_MOD)
                if c:
                    normalize("I", c - 1, x0[:, c - 1])
                if c == 1:
                    modulation()
            normalize("I", CH - 1, x0[:, CH - 1])

            def slot(s, c, l, extra=None):
                a, b, f, d = s, s - 1, s - 2, s - 3
                if has(f):
                    dve.wait_ge(to_fm["B"], f + 1)
                    if (c - 2) % CH == 0:
                        dve.wait_ge(ld["vln1"], 4 * f + 16)
                    for h in range(HB):
                        nc.vector.tensor_scalar(half(x2[(c - 2) % CH], h), half(ps_b, h), vln1[:, 0:1], vln1[:, 1:2],
                                                ALU.mult, ALU.add).then_inc(x2_ready, 1)
                if has(b):
                    dve.wait_ge(nck_ready, b + 1)
                    dve.wait_ge(dd_ready, b + 1)
                    for h in range(HB):
                        vv = nc.vector.tensor_scalar(half(vt[(c - 1) % CH], h), half(dd, h), nck[:, h:h + 1],
                                                     ck[:, h:h + 1], ALU.mult, ALU.add)
                    vv.then_inc(v_ready, 1)
                run(extra, "before the last norm")
                if has(d):
                    dve.wait_ge(to_tm["D"], d + 1)
                    stats("D", d, tiles(ps_d), EPS_LN)
                if has(a):
                    if c == 0:
                        dve.wait_ge(ld["va"], 16 * l + 16)
                    dve.wait_ge(ek_ready, a + 1)
                    nc.vector.tensor_scalar(mk[:], ek[:], 1.0, -1.0, ALU.min, ALU.add).then_inc(mk_ready, 1)
                    dve.wait_ge(mk_ready, a + 1)
                    nc.vector.scalar_tensor_tensor(out=elu_k_sb[:], in0=ps_k[:], scalar=va[:, 0:1], in1=mk[:],
                                                   op0=ALU.add, op1=ALU.max).then_inc(elu_k, 1)
                if has(d):
                    normalize("D", d, tiles(ps_d))
                run(extra, "after the last norm")
                if has(a):
                    dve.wait_ge(eq_ready, a + 1)
                    nc.vector.tensor_scalar(mq[:], eq[:], 1.0, -1.0, ALU.min, ALU.add).then_inc(mq_ready, 1)
                    dve.wait_ge(elu_k, a + 1)
                    for h in range(HB):
                        kh = nc.vector.tensor_scalar(half(kk, h), half(elu_k_sb, h), 1.0, None, ALU.add, ALU.add,
                                                     accum_out=ksum[:, h:h + 1])
                    kh.then_inc(k_ready, 1)
                    dve.wait_ge(mq_ready, a + 1)
                    nc.vector.scalar_tensor_tensor(out=elu_q_sb[:], in0=ps_q[:], scalar=va[:, 1:2], in1=mq[:],
                                                   op0=ALU.add, op1=ALU.max).then_inc(elu_q, 1)
                if has(b):
                    dve.wait_ge(to_tm["B"], b + 1)
                    stats("B", b, tiles(ps_b), EPS_LN)
                if has(a):
                    dve.wait_ge(k_ready, a + 1)
                    nc.vector.tensor_scalar(kpos[:], ksum[:], 1e-30, None, ALU.max).then_inc(kpos_ready, 1)
                    dve.wait_ge(v_mm, a + 1)
                    for h in range(HB):
                        kv = nc.vector.scalar_tensor_tensor(out=half(kv_full, h), in0=half(ps_v, h), scalar=va[:, 2:3],
                                                            in1=half(kk, h), op0=ALU.add, op1=ALU.mult,
                                                            accum_out=kvsum[:, h:h + 1])
                    kv.then_inc(kv_ready, 1)
                    dve.wait_ge(kpos_ready, a + 1)
                    nc.vector.reciprocal(rk[:], kpos[:]).then_inc(rk_ready, 1)
                run(extra, "within the first norm")
                if has(b):
                    normalize("B", b, tiles(ps_b))
                if has(a):
                    dve.wait_ge(kv_ready, a + 1)
                    dve.wait_ge(rk_ready, a + 1)
                    nc.vector.tensor_tensor(ck[:], kvsum[:], rk[:], ALU.mult).then_inc(ck_ready, 1)
                    dve.wait_ge(ck_ready, a + 1)
                    nc.vector.tensor_scalar(nck[:], ck[:], -1.0, None, ALU.mult).then_inc(nck_ready, 1)

            slots(dve, slot)

            STEPS = 12

            def step(n, op):
                op.then_inc(rt, 1)
                dve.wait_ge(rt, n)

            def scaled(c):
                dve.wait_ge(x_ready, NI + c + 1)
                for h in range(HB):
                    b = c * HB + h
                    z = nc.vector.tensor_scalar(half(zf, h), half(xs[c], h), gt[:, 0, b:b + 1], None, ALU.mult)
                z.then_inc(zf_ready, 1)

            def residual(c):
                dve.wait_ge(to_tm["F"], c + 1)
                nc.vector.tensor_tensor(x0[:, c], tiles(ps_q), x0[:, c], ALU.add).then_inc(x_new, 1)

            def residual_stats(c):
                dve.wait_ge(x_new, c + 1)
                stats("F", c, x0[:, c], EPS_MOD)

            def second_norm(c):
                if c:
                    dve.wait_ge(to_fm["F"], c)
                normalize("F", c, x0[:, c])

            own = lg[:].unsqueeze(3).to_broadcast([P, T, E, E])
            other = lg[:].unsqueeze(2).to_broadcast([P, T, E, E])
            low = lower[:].rearrange("p (a b) -> p a b", a=E).unsqueeze(1).to_broadcast([P, T, E, E])

            def v4(t):
                return t[:].rearrange("p t (a b) -> p t a b", a=E)

            def route_scores(c):
                n = STEPS * c
                dve.wait_ge(score_mm, c + 1)
                score = ps_q[:, 0:T * E].rearrange("p (t e) -> p t e", t=T)
                step(n + 1, nc.vector.tensor_reduce(mx[:], score, AX_X, ALU.max))
                nc.vector.tensor_tensor(lg[:], score, mx[:].unsqueeze(2).to_broadcast([P, T, E]),
                                        ALU.subtract).then_inc(lg_ready, 1)
                dve.wait_ge(lg_ready, c + 1)
                nc.vector.tensor_tensor(v4(cmp_gt), other, own, ALU.is_gt)
                step(n + 2, nc.vector.tensor_tensor(v4(cmp_eq), other, own, ALU.is_equal))

            def route_compare(c):
                n = STEPS * c
                step(n + 3, nc.vector.tensor_tensor(v4(cmp_lo), v4(cmp_eq), low, ALU.mult))
                step(n + 4, nc.vector.tensor_tensor(cmp_all[:], cmp_gt[:], cmp_lo[:], ALU.add))

            def route_ranks(c):
                n = STEPS * c
                step(n + 5, nc.vector.tensor_reduce(rank[:], v4(cmp_all), AX_X, ALU.add))
                dve.wait_ge(ex_ready, c + 1)
                step(n + 6, nc.vector.tensor_reduce(sm[:], ex[:], AX_X, ALU.add))
                nc.vector.reciprocal(rsm[:], sm[:])
                step(n + 7, nc.vector.scalar_tensor_tensor(out=comb[:], in0=rank[:], scalar=1.5, in1=ex[:],
                                                           op0=ALU.is_lt, op1=ALU.mult))

            def route_weights(c):
                n = STEPS * c
                step(n + 8, nc.vector.tensor_tensor(comb2[:], comb[:], rsm[:].unsqueeze(2).to_broadcast([P, T, E]),
                                                    ALU.mult))
                if c:
                    dve.wait_ge(cst_mm, c)
                step(n + 9, nc.vector.tensor_copy(cs[:, :, 0, :], comb2[:]))
                step(n + 10, nc.vector.tensor_tensor(res1[:], comb2[:], cs[:, :, 0, :], ALU.subtract))
                step(n + 11, nc.vector.tensor_copy(cs[:, :, 1, :], res1[:]))
                step(n + 12, nc.vector.tensor_tensor(res2[:], res1[:], cs[:, :, 1, :], ALU.subtract))
                nc.vector.tensor_copy(cs[:, :, 2, :], res2[:]).then_inc(cs_ready, 1)

            def mixture_sum(c):
                dve.wait_ge(down_mm, (c + 1) * U)
                for h in range(HB):
                    b = c * HB + h
                    nc.vector.tensor_scalar(half(yf, h), half(ps_y, h), gt[:, 1, b:b + 1], None,
                                            ALU.mult).then_inc(yf_ready, 1)

            def result(c):
                dve.wait_ge(out_tm, c + 1)
                if c >= 2:
                    dve.wait_ge(stored[c % 2], 16 * (c // 2))
                nc.vector.tensor_tensor(ot[c % 2][:], tiles(ps_q), x0[:, c], ALU.add).then_inc(ot_ready, 1)

            def consts_and_scores_0():
                dve.wait_ge(ld["moe"], MOE_LOADS)
                nc.vector.tensor_copy(identb[:], ident[:]).then_inc(moe_consts, 1)
                route_scores(0)

            def residual_0():
                residual(0)
                residual_stats(0)

            scaled(0)
            slot(NI, 0, LAYERS, {"after the last norm": residual_0, "within the first norm": lambda: second_norm(0)})
            slot(NI + 1, 1, LAYERS, {"before the last norm": consts_and_scores_0})
            nc.vector.tensor_copy(sel[:], sel32[:]).then_inc(moe_consts, 1)
            route_compare(0)
            route_ranks(0)
            route_weights(0)
            for i in range(CH * U):
                c, u = divmod(i, U)
                n = c + 1
                if n < CH:
                    if u == 1:
                        scaled(n)
                    if u == 3:
                        residual(n)
                    if u == 4:
                        residual_stats(n)
                    if u == 5:
                        second_norm(n)
                    if u == 8:
                        route_compare(n)
                    if u == 9:
                        route_ranks(n)
                if u == 0 and c:
                    route_weights(c)
                if i == U + 2:
                    dve.wait_ge(to_tm["D"], NI)
                    stats("D", NI - 1, tiles(ps_v), EPS_LN)
                if i == U + 3:
                    normalize("D", NI - 1, tiles(ps_v))
                dve.wait_ge(sg_ready, i + 1)
                dve.wait_ge(up_mm, i + 1)
                if i >= 3:
                    dve.wait_ge(down_mm, i - 2)
                    if splits(i - 2) > splits(i - 3):
                        dve.wait_ge(sc_lo_ready, splits(i - 2))
                if u >= SHARED:
                    nc.vector.tensor_tensor(su[i % 2][:], up_bank[i % 2][:], sg[i % 2][:], ALU.mult).then_inc(su_ready, 1)
                    dve.wait_ge(su_ready, i + 1)
                    dve.wait_ge(bc_mm, routed(i) + 1)
                    nc.vector.tensor_tensor(sc[i % 3][:], ps_d[:], su[i % 2][:], ALU.mult).then_inc(sc_ready, 1)
                else:
                    nc.vector.tensor_tensor(sc[i % 3][:], up_bank[i % 2][:], sg[i % 2][:], ALU.mult).then_inc(su_ready, 1)
                if u == 1 and c:
                    mixture_sum(c - 1)
                if u == 7 and n < CH:
                    route_scores(n)
                if u == 5 and c:
                    result(c - 1)
            mixture_sum(CH - 1)
            result(CH - 1)


def kernel(**inputs):
    import numpy as np
    import concourse.bacc as bacc
    from concourse.bass_utils import run_bass_kernel_spmd

    def w(name):
        return np.asarray(inputs[name])

    def stack(*names):
        return np.ascontiguousarray(np.stack([w(n) for n in names], axis=-1))

    select = np.zeros((3, E, E, P), np.float32)
    for e in range(E):
        select[:, e, e, :] = 1.0
    lower = np.broadcast_to(np.tril(np.ones((E, E), np.float32), -1).reshape(1, E * E), (P, E * E))
    sg = w("L0_ffn_shared_gate_w").reshape(D, 2, P)
    su = w("L0_ffn_shared_up_w").reshape(D, 2, P)
    sd = w("L0_ffn_shared_down_w").reshape(2, P, D).transpose(1, 0, 2)
    gates = np.concatenate([sg, w("L0_ffn_gate_w").transpose(1, 0, 2)], axis=1)
    ups = np.concatenate([su, w("L0_ffn_up_w").transpose(1, 0, 2)], axis=1)
    downs = np.concatenate([sd, w("L0_ffn_down_w").transpose(1, 0, 2)], axis=1)
    arrays = {
        "x": w("L0_attn_x").reshape(NB * L, D),
        "w_qkv": np.concatenate([w("L0_attn_Wk"), w("L0_attn_Wq"), w("L0_attn_Wv")], axis=2),
        "w_o": w("L0_attn_Wo"),
        "w_f1": w("L0_attn_Wf1"),
        "w_f2": w("L0_attn_Wf2").reshape(LAYERS, FJ, P, D).transpose(0, 2, 1, 3),
        "v_a": stack("L0_attn_bk", "L0_attn_bq", "L0_attn_bv"),
        "v_bo": stack("L0_attn_bo"),
        "v_ln1": stack("L0_attn_ln1_s", "L0_attn_ln1_b"),
        "v_bf1": w("L0_attn_bf1").reshape(LAYERS, FJ, P).transpose(0, 2, 1),
        "v_bf2": stack("L0_attn_bf2"),
        "v_ln2": stack("L0_attn_ln2_s", "L0_attn_ln2_b"),
        "c_t": w("L0_c").T,
        "w_mod": w("L0_wmod"),
        "w_router": w("L0_ffn_router_w"),
        "w_unit": np.stack([gates, ups, downs], axis=2),
        "ident": np.eye(P, dtype=np.float32),
        "select": select.reshape(3 * E, E * P),
        "lower": lower,
    }
    nc = bacc.Bacc("TRN2", target_bir_lowering=False, num_devices=1)
    arrays = {f"in_{k}": np.ascontiguousarray(a) for k, a in arrays.items()}
    args = [nc.dram_tensor(k, a.shape, mybir.dt.from_np(a.dtype), kind="ExternalInput").ap() for k, a in arrays.items()]
    result = nc.dram_tensor("out_0", (NB * L, D), F32, kind="ExternalOutput").ap()
    adaln_block(nc, *args, result)
    r = run_bass_kernel_spmd(nc, [arrays], core_ids=[0])
    return r.results[0]["out_0"].reshape(NB, L, D)
```
